# Optimizing a Trainium2 kernel written in Bass

```python
import numpy as np
import jax
import jax.numpy as jnp

def _softmax(x, axis=-1):
    return jax.nn.softmax(x, axis=axis)
def _gelu(x):
    return jax.nn.gelu(x, approximate=True)
def _silu(x):
    return jax.nn.silu(x)
def _sigmoid(x):
    return jax.nn.sigmoid(x)
def _layernorm(x, axis=-1, eps=1e-5):
    m = jnp.mean(x, axis=axis, keepdims=True)
    v = jnp.var(x, axis=axis, keepdims=True)
    return (x - m) / jnp.sqrt(v + eps)
def _scatter_add(tgt, idx, src, axis=0):
    return tgt.at[idx].add(src)
def _segment_sum(src, seg, n):
    return jax.ops.segment_sum(src, seg, n)

kernel_name = 'mk_conv_preact_d1_conv_nchw512_483e7f'

def setup_inputs(seed: int = 0):
    np.random.seed(seed)
    _w = jnp.asarray
    def _rec_inputs():
        import jax
        import jax.numpy as jnp
        _gk = jax.random.key(seed)
        x = -0.0006322 + 1.001 * jax.random.normal(jax.random.fold_in(_gk, 1), (2, 512, 53, 53), jnp.float32)
        return x
    x = _rec_inputs()
    def _L0_conv_setup():
        import jax, jax.numpy as jnp
        import numpy as np
        B, C, H, W = (2, 512, 53, 53)
        N_HEADS = 8
        D_HEAD = C // N_HEADS
        key = jax.random.key(seed)
        k1, k2, k3, k4 = jax.random.split(key, 4)
        scale = D_HEAD ** (-0.5)
        return {'x': jax.random.normal(k1, (B, C, H, W), dtype=jnp.float32), 'w_in': jax.random.normal(k2, (3 * C, C), dtype=jnp.float32) * 0.02, 'pos_h': jax.random.normal(k3, (H, D_HEAD), dtype=jnp.float32) * scale, 'pos_w': jax.random.normal(k4, (W, D_HEAD), dtype=jnp.float32) * scale}
    _L0_conv_all = _L0_conv_setup()
    _L0_conv_in = {k: v for k, v in _L0_conv_all.items() if k in ('w_in', 'pos_h', 'pos_w', )}
    del _L0_conv_all

    return {
        "x": x,
        "L0_conv_w_in": _L0_conv_in["w_in"],
        "L0_conv_pos_h": _L0_conv_in["pos_h"],
        "L0_conv_pos_w": _L0_conv_in["pos_w"],
    }

def reference(x, L0_conv_w_in, L0_conv_pos_h, L0_conv_pos_w):
    import jax
    import jax.numpy as jnp
    def _L0_conv_ref(x, w_in, pos_h, pos_w):
        import jax, jax.numpy as jnp
        import numpy as np
        B, C, H, W = (2, 512, 53, 53)
        N_HEADS = 8
        D_HEAD = C // N_HEADS
        b, c, h, w = x.shape
        n, d = (N_HEADS, c // N_HEADS)
        hw = h * w
        qkv = jnp.einsum('bchw,oc->bohw', x, w_in)
        q, k, v = jnp.split(qkv, 3, axis=1)

        def to_heads(t):
            return t.reshape(b, n, d, hw).transpose(0, 1, 3, 2)
        q, k, v = (to_heads(q), to_heads(k), to_heads(v))
        scale = jnp.sqrt(jnp.asarray(d, dtype=x.dtype))
        sim = jnp.einsum('bhid,bhjd->bhij', q, k) * scale
        emb = (pos_h[:, None, :] + pos_w[None, :, :]).reshape(hw, d)
        sim = sim + jnp.einsum('bhid,jd->bhij', q, emb) * d ** (-0.5)
        attn = jax.nn.softmax(sim, axis=-1)
        out = jnp.einsum('bhij,bhjd->bhid', attn, v)
        return out.transpose(0, 1, 3, 2).reshape(b, c, h, w)

    def _gn(v, G=32, eps=1e-5):
        B_, C_, H_, W_ = v.shape
        g = v.reshape(B_, G, C_ // G, H_, W_)
        m = jnp.mean(g, axis=(2, 3, 4), keepdims=True)
        s = jnp.var(g, axis=(2, 3, 4), keepdims=True)
        return ((g - m) / jnp.sqrt(s + eps)).reshape(v.shape)

    def _ln_c(v, eps=1e-6):
        m = jnp.mean(v, axis=1, keepdims=True)
        s = jnp.var(v, axis=1, keepdims=True)
        return (v - m) / jnp.sqrt(s + eps)

    def _ln_t(v, eps=1e-5):
        m = jnp.mean(v, axis=-1, keepdims=True)
        s = jnp.var(v, axis=-1, keepdims=True)
        return (v - m) / jnp.sqrt(s + eps)

    def _to_tokens(v):
        B_, C_, H_, W_ = v.shape
        return v.reshape(B_, C_, H_ * W_).transpose(0, 2, 1)
    def _from_tokens(t, like):
        B_, C_, H_, W_ = like.shape
        return t.transpose(0, 2, 1).reshape(B_, C_, H_, W_)

    x = x + _L0_conv_ref(_gn(x), L0_conv_w_in, L0_conv_pos_h, L0_conv_pos_w)
    return x


_drawn_inputs = setup_inputs


def setup_inputs(seed=0):
    import zlib

    import numpy as np

    out = dict(_drawn_inputs(seed))
    spreads = {}
    factors = {'L0_conv_pos_h': 8.0, 'L0_conv_pos_w': 8.0}
    for name, (base, spread) in spreads.items():
        noise = np.random.default_rng([zlib.crc32(name.encode()), seed]).standard_normal(out[name].shape)
        drawn = base * np.exp(spread * noise) if base else spread * noise
        out[name] = jnp.asarray(drawn.astype(out[name].dtype))
    for name, factor in factors.items():
        out[name] = (out[name] * factor).astype(out[name].dtype)
    return out
```

```python
import concourse.bass as bass
from concourse import mybir
from contextlib import ExitStack
import numpy as np

B, C, H, W = 2, 512, 53, 53
HEADS = 8
D = C // HEADS
T = H * W
P = 128
CB = C // P
PAIRS = B * CB
GROUP = C // 32
GN_EPS = 1e-5

KT = -(-T // P)
TP = KT * P
LAST_KEYS = T - (KT - 1) * P
UNITS = 3
QH = 470
QB = 2 * QH
TQ = UNITS * QB

MAX_CHUNKS = -(-T // QH)
CHUNKS_A_STEP = MAX_CHUNKS // 3
LEAD = 27
LAG = 3

XC = 256
NXC = TP // XC
VT = XC // P

F32 = mybir.dt.float32
F32R = mybir.dt.float32r
ALU = mybir.AluOpType
ACT = mybir.ActivationFunctionType
AX = mybir.AxisListType


def clear_semaphores(nc, sems):
    for s in sems:
        nc.sync.sem_clear(s)
    nc.all_engine_barrier()


def project(nc, x, w_t, pos_h_t, pos_w_t, group_mean, q_hi_d, q_lo_d, k_hi_d, k_lo_d, v_d):
    with ExitStack() as ctx:
        def sb(name, shape, dt=F32):
            return ctx.enter_context(nc.sbuf_tensor(name, shape, dt))

        def ps(name, shape):
            return ctx.enter_context(nc.psum_tensor(name, shape, F32))

        made = []

        def sem(name):
            made.append(ctx.enter_context(nc.semaphore(name)))
            return made[-1]

        xs = sb("x_sb", [P, B, CB, TP])
        w32 = sb("w32", [P, 1, 3 * C])
        w_hi = sb("w_hi", [P, CB, 3 * C], F32R)
        w_lo = sb("w_lo", [P, CB, 3 * C], F32R)
        pos_h = sb("pos_h", [P, H])
        pos_w = sb("pos_w", [P, W])
        emb = sb("emb", [P, 1, TP])
        avg = sb("avg", [P, P])
        NST = -(-T // 512)
        stats = sb("stats", [P, B * CB, NST, 6])
        mv = sb("mv", [P, B * CB, 2])
        g_mean = sb("g_mean", [P, B * CB])
        dev = sb("dev", [P, B * CB])
        dev2 = sb("dev2", [P, B * CB])
        var_e = sb("var_e", [P, B * CB])
        std = sb("std", [P, B * CB])
        r0 = sb("r0", [P, B * CB])
        r1 = sb("r1", [P, B * CB])
        r2 = sb("r2", [P, B * CB])
        g_rstd = sb("g_rstd", [P, B * CB])
        mean_b = sb("mean_b", [P, CB])
        rstd_b = sb("rstd_b", [P, CB])
        xn = sb("xn", [P, CB, XC])
        xn_hi = sb("xn_hi", [P, 2, CB, XC], F32R)
        xn_lo = sb("xn_lo", [P, 2, CB, XC], F32R)
        q_hi = sb("q_hi", [P, CB, XC], F32R)
        q_lo = sb("q_lo", [P, CB, XC], F32R)
        k_sum = sb("k_sum", [P, CB, XC])
        k_hi = sb("k_hi", [P, CB, XC], F32R)
        k_lo = sb("k_lo", [P, CB, XC], F32R)
        v_parts = sb("v_parts", [P, VT, HEADS, 2, D], F32R)

        q_ps = ps("q_ps", [P, CB, XC])
        k_ps = ps("k_ps", [P, CB, XC])
        v_ps = ps("v_ps", [P, VT, C])
        stat_ps = ps("stat_ps", [P, 512])

        x_loaded = [sem(f"x{n}_loaded") for n in range(B * CB)]
        small_loaded = sem("small_loaded")
        w_loaded = sem("w_loaded")
        w_hi_ready = sem("w_hi_ready")
        w_lo_ready = sem("w_lo_ready")
        stat_ready = sem("stat_ready")
        stat_summed = sem("stat_summed")
        std_ready = sem("std_ready")
        chain = sem("dve_chain")

        with nc.Block() as block:
            @block.sync
            def _(sp):
                for b in range(B):
                    for c in range(CB):
                        sp.dma_start(xs[:, b, c, 0:T], x[b * CB + c, :, :]).then_inc(x_loaded[b * CB + c], 16)
                        if b == 0 and c == 0:
                            for half in range(2):
                                rows = slice(half * D, (half + 1) * D)
                                sp.dma_start(pos_h[rows, :], pos_h_t[:, :]).then_inc(small_loaded, 16)
                                sp.dma_start(pos_w[rows, :], pos_w_t[:, :]).then_inc(small_loaded, 16)
                            sp.dma_start(avg[:, :], group_mean[:, :]).then_inc(small_loaded, 16)

            @block.scalar
            def _(act):
                for c in range(CB):
                    if c:
                        act.wait_ge(w_lo_ready, c)
                    act.dma_start(w32[:, 0, :], w_t[c * P:(c + 1) * P, :]).then_inc(w_loaded, 16)
                    act.wait_ge(w_loaded, 16 * (c + 1))
                    nc.scalar.copy(w_hi[:, c, :], w32[:, 0, :]).then_inc(w_hi_ready, 1)
                act.wait_ge(stat_ready, 3)
                nc.scalar.activation(std[:, :], var_e[:, :], ACT.Sqrt).then_inc(std_ready, 1)

            @block.gpsimd
            def _(pool):
                nc.gpsimd.memset(xs[:, :, :, T:TP], 0.0)
                nc.gpsimd.memset(emb[:, :, T:TP], 0.0)
                for c in range(CB):
                    pool.wait_ge(w_hi_ready, c + 1)
                    nc.gpsimd.tensor_tensor(w_lo[:, c, :], w32[:, 0, :], w_hi[:, c, :].bitcast(F32),
                                            ALU.subtract).then_inc(w_lo_ready, 1)

            @block.tensor
            def _(pe):
                pe.wait_ge(small_loaded, 16 * 5)
                pe.wait_ge(stat_ready, 1)
                nc.tensor.matmul(stat_ps[:, 0:B * CB], avg[:, :], mv[:, :, 0],
                                 start=True, stop=True).then_inc(stat_summed, 1)
                pe.wait_ge(stat_ready, 2)
                nc.tensor.matmul(stat_ps[:, 0:B * CB], avg[:, :], dev2[:, :],
                                 start=True, stop=True).then_inc(stat_summed, 1)

            @block.vector
            def _(dve):
                links = [0]

                def link(ins):
                    links[0] += 1
                    ins.then_inc(chain, 1)
                    dve.wait_ge(chain, links[0])

                dve.wait_ge(small_loaded, 16 * 5)
                nc.vector.tensor_scalar(pos_h[:, :], pos_h[:, :], 1.0 / D, None, ALU.mult)
                link(nc.vector.tensor_scalar(pos_w[:, :], pos_w[:, :], 1.0 / D, None, ALU.mult))
                nc.vector.tensor_tensor(emb[:, 0, 0:T].rearrange("p (i j) -> p i j", j=W),
                                        pos_h[:, :].unsqueeze(2).broadcast_to([P, H, W]),
                                        pos_w[:, :].unsqueeze(1).broadcast_to([P, H, W]), ALU.add)
                for n in range(B * CB):
                    dve.wait_ge(x_loaded[n], 16)
                    for s in range(NST):
                        hi = min(T, (s + 1) * 512)
                        last = nc.vector.bn_stats(stats[:, n, s, :], xs[:, n // CB, n % CB, s * 512:hi])
                    link(last)
                    last = nc.vector.bn_aggr(mv[:, n, :], stats[:, n, :, :])
                last.then_inc(stat_ready, 1)
                dve.wait_ge(stat_summed, 1)
                link(nc.vector.tensor_copy(g_mean[:, :], stat_ps[:, 0:B * CB]))
                link(nc.vector.tensor_tensor(dev[:, :], mv[:, :, 0], g_mean[:, :], ALU.subtract))
                link(nc.vector.tensor_tensor(dev[:, :], dev[:, :], dev[:, :], ALU.mult))
                nc.vector.tensor_tensor(dev2[:, :], mv[:, :, 1], dev[:, :], ALU.add).then_inc(stat_ready, 1)
                dve.wait_ge(stat_summed, 2)
                nc.vector.tensor_scalar(var_e[:, :], stat_ps[:, 0:B * CB], GN_EPS, None,
                                        ALU.add).then_inc(stat_ready, 1)
                dve.wait_ge(std_ready, 1)
                link(nc.vector.reciprocal(r0[:, :], std[:, :]))
                link(nc.vector.tensor_tensor(r1[:, :], r0[:, :], r0[:, :], ALU.mult))
                link(nc.vector.tensor_tensor(r2[:, :], r1[:, :], var_e[:, :], ALU.mult))
                link(nc.vector.tensor_scalar(r1[:, :], r2[:, :], -0.5, 1.5, ALU.mult, ALU.add))
                nc.vector.tensor_tensor(g_rstd[:, :], r0[:, :], r1[:, :], ALU.mult)

        clear_semaphores(nc, made)

        ab_ready = sem("affine_ready")
        xn_ready = sem("xn_ready")
        xhi_ready = sem("xn_hi_ready")
        xlo_ready = sem("xn_lo_ready")
        q_made = sem("q_made")
        k_made = sem("k_made")
        v_made = sem("v_made")
        qhi_ready = sem("q_hi_ready")
        qlo_ready = sem("q_lo_ready")
        ksum_ready = sem("k_sum_ready")
        khi_ready = sem("k_hi_ready")
        klo_ready = sem("k_lo_ready")
        vhi_ready = sem("v_hi_ready")
        vlo_ready = sem("v_lo_ready")
        q_stored = sem("q_stored")
        k_stored = sem("k_stored")
        v_stored = sem("v_stored")
        loop_sems = made[-18:]

        with nc.Fori(0, B) as b:
            with nc.Block() as block:
                @block.sync
                def _(sp):
                    for i in range(NXC):
                        at = slice(i * XC, (i + 1) * XC)
                        sp.wait_ge(qlo_ready, i + 1)
                        sp.dma_start(q_hi_d[bass.ds(b * CB, CB), :, at].rearrange("m p t -> p m t"),
                                     q_hi[:, :, :].bitcast(F32)).then_inc(q_stored, 16)
                        sp.dma_start(q_lo_d[bass.ds(b * CB, CB), :, at].rearrange("m p t -> p m t"),
                                     q_lo[:, :, :].bitcast(F32)).then_inc(q_stored, 16)
                        sp.wait_ge(klo_ready, i + 1)
                        sp.dma_start(k_hi_d[bass.ds(b * CB, CB), :, at].rearrange("m p t -> p m t"),
                                     k_hi[:, :, :].bitcast(F32)).then_inc(k_stored, 16)
                        sp.dma_start(k_lo_d[bass.ds(b * CB, CB), :, at].rearrange("m p t -> p m t"),
                                     k_lo[:, :, :].bitcast(F32)).then_inc(k_stored, 16)
                        sp.wait_ge(vlo_ready, i + 1)
                        for t in range(VT):
                            sp.dma_start(v_d[bass.ds(b * CB, CB), i * VT + t, :, :].rearrange("m p n -> p m n"),
                                         v_parts[:, t, :, :, :].bitcast(F32).rearrange("p (m h) s d -> p m (h s d)", m=CB)
                                         ).then_inc(v_stored, 16)
                    sp.wait_ge(q_stored, 32 * NXC)
                    sp.wait_ge(k_stored, 32 * NXC)
                    sp.wait_ge(v_stored, 16 * VT * NXC)

                @block.vector
                def _(dve):
                    nc.vector.tensor_copy(mean_b[:, :], g_mean[:, bass.ds(b * CB, CB)]).then_inc(ab_ready, 1)
                    nc.vector.tensor_copy(rstd_b[:, :], g_rstd[:, bass.ds(b * CB, CB)]).then_inc(ab_ready, 1)
                    dve.wait_ge(ab_ready, 2)

                    def normalise(i):
                        if i >= 1:
                            dve.wait_ge(xlo_ready, i)
                        for c in range(CB):
                            last = nc.vector.tensor_scalar(
                                xn[:, c, :], xs[:, bass.ds(b, 1), c, i * XC:(i + 1) * XC],
                                mean_b[:, c:c + 1], rstd_b[:, c:c + 1], ALU.subtract, ALU.mult)
                        last.then_inc(xn_ready, 1)
                        dve.wait_ge(xhi_ready, i + 1)
                        nc.vector.tensor_tensor(xn_lo[:, i % 2, :, :], xn[:, :, :],
                                                xn_hi[:, i % 2, :, :].bitcast(F32),
                                                ALU.subtract).then_inc(xlo_ready, 1)

                    normalise(0)
                    for i in range(NXC):
                        if i + 1 < NXC:
                            if i >= 1:
                                dve.wait_ge(v_made, i)
                            normalise(i + 1)
                        dve.wait_ge(qhi_ready, i + 1)
                        nc.vector.tensor_tensor(q_lo[:, :, :], q_ps[:, :, :], q_hi[:, :, :].bitcast(F32),
                                                ALU.subtract).then_inc(qlo_ready, 1)
                        dve.wait_ge(k_made, i + 1)
                        if i >= 1:
                            dve.wait_ge(klo_ready, i)
                        nc.vector.tensor_tensor(
                            k_sum[:, :, :], k_ps[:, :, :],
                            emb[:, :, i * XC:(i + 1) * XC].broadcast_to([P, CB, XC]),
                            ALU.add).then_inc(ksum_ready, 1)
                        dve.wait_ge(vhi_ready, i + 1)
                        nc.vector.tensor_tensor(
                            v_parts[:, :, :, 1, :],
                            v_ps[:, :, :].rearrange("p t (h d) -> p t h d", d=D),
                            v_parts[:, :, :, 0, :].bitcast(F32), ALU.subtract).then_inc(vlo_ready, 1)

                @block.scalar
                def _(act):
                    def round_x(i):
                        act.wait_ge(xn_ready, i + 1)
                        nc.scalar.copy(xn_hi[:, i % 2, :, :], xn[:, :, :]).then_inc(xhi_ready, 1)

                    round_x(0)
                    for i in range(NXC):
                        if i + 1 < NXC:
                            round_x(i + 1)
                        act.wait_ge(q_made, i + 1)
                        if i >= 1:
                            act.wait_ge(q_stored, 32 * i)
                        nc.scalar.copy(q_hi[:, :, :], q_ps[:, :, :]).then_inc(qhi_ready, 1)
                        act.wait_ge(ksum_ready, i + 1)
                        if i >= 1:
                            act.wait_ge(k_stored, 32 * i)
                        nc.scalar.copy(k_hi[:, :, :], k_sum[:, :, :]).then_inc(khi_ready, 1)
                        act.wait_ge(v_made, i + 1)
                        if i >= 1:
                            act.wait_ge(v_stored, 16 * VT * i)
                        nc.scalar.copy(v_parts[:, :, :, 0, :],
                                       v_ps[:, :, :].rearrange("p t (h d) -> p t h d", d=D)
                                       ).then_inc(vhi_ready, 1)

                @block.gpsimd
                def _(pool):
                    for i in range(NXC):
                        pool.wait_ge(khi_ready, i + 1)
                        nc.gpsimd.tensor_tensor(k_lo[:, :, :], k_sum[:, :, :], k_hi[:, :, :].bitcast(F32),
                                                ALU.subtract).then_inc(klo_ready, 1)

                @block.tensor
                def _(pe):
                    terms = [(c, w, xp) for c in range(CB)
                             for w, xp in ((w_hi, xn_hi), (w_lo, xn_hi), (w_hi, xn_lo))]

                    def channels(out, o0, i):
                        for n, (c, w, xp) in enumerate(terms):
                            last = nc.tensor.matmul(out, w[:, c, o0:o0 + P], xp[:, i % 2, c, :],
                                                    start=(n == 0), stop=(n == len(terms) - 1))
                        return last

                    for i in range(NXC):
                        pe.wait_ge(xlo_ready, i + 1)
                        if i >= 1:
                            pe.wait_ge(qlo_ready, i)
                        for m in range(CB):
                            last = channels(q_ps[:, m, :], m * P, i)
                        last.then_inc(q_made, 1)
                        if i >= 1:
                            pe.wait_ge(ksum_ready, i)
                        for m in range(CB):
                            last = channels(k_ps[:, m, :], C + m * P, i)
                        last.then_inc(k_made, 1)
                        if i >= 1:
                            pe.wait_ge(vlo_ready, i)
                        for t in range(VT):
                            for n, (c, w, xp) in enumerate(terms):
                                last = nc.tensor.matmul(v_ps[:, t, :], xp[:, i % 2, c, t * P:(t + 1) * P],
                                                        w[:, c, 2 * C:3 * C],
                                                        start=(n == 0), stop=(n == len(terms) - 1))
                        last.then_inc(v_made, 1)

            clear_semaphores(nc, loop_sems)



HEAD_STEPS = UNITS * KT
STEPS = 2 * HEAD_STEPS
FIRST_TILE = LEAD // 3
END_TILE = FIRST_TILE + STEPS // 3
NP, NHI, NLO = 3, 4, 3


def keys_of(kt):
    return LAST_KEYS if kt == KT - 1 else P


def sums_through(g):
    unit, kt = divmod(g, KT)
    return unit * (KT - 1) + max(kt, 1)


def ring_order(steps):
    plan = []
    for g in steps:
        jobs = []
        tile, third = divmod(g + LEAD, 3)
        if tile < END_TILE:
            jobs += [("chunk", tile, CHUNKS_A_STEP * third + n) for n in range(CHUNKS_A_STEP)]
        if third == 1 and FIRST_TILE <= tile - 1 < END_TILE:
            jobs.append(("row", tile - 1, 0))
        unit, kt = divmod(g, KT)
        unit -= 1
        if 0 <= unit < 2 * UNITS:
            if kt in (3, 4):
                jobs.append(("total", unit, kt - 3))
            if kt in (6, 7):
                jobs.append(("output", unit, kt - 6))
        plan.append(jobs)
    return plan


TAIL = 8
PLAN = ring_order(range(STEPS + TAIL))


def ring_positions(plan):
    order = [job for jobs in plan for job in jobs]
    vector = [0]
    scalar = [0]
    for kind, _, _ in order:
        vector.append(vector[-1] + (kind != "row"))
        scalar.append(scalar[-1] + (kind == "row"))
    return order, vector, scalar


def attend(nc, x, out, identity, q_hi_d, q_lo_d, k_hi_d, k_lo_d, v_d):
    with ExitStack() as ctx:
        def sb(name, shape, dt=F32):
            return ctx.enter_context(nc.sbuf_tensor(name, shape, dt))

        def ps(name, shape):
            return ctx.enter_context(nc.psum_tensor(name, shape, F32))

        made = []

        def sem(name):
            made.append(ctx.enter_context(nc.semaphore(name)))
            return made[-1]

        k_parts = [sb(f"k_parts{h}", [P, TP], F32R) for h in range(2)]
        k_one = [sb(f"k_one{h}", [D + 1, TP], F32R) for h in range(2)]
        q_twice = [sb(f"q_twice{h}", [P, TQ], F32R) for h in range(2)]
        q_max = [sb(f"q_max{h}", [D + 1, TQ], F32R) for h in range(2)]
        v_parts = [sb(f"v_parts{h}", [P, KT, 2 * D], F32R) for h in range(2)]
        probs = sb("probs", [P, NP, QB])
        p_hi = sb("p_hi", [P, NHI, QB], F32R)
        p_lo = sb("p_lo", [P, NLO, QB], F32R)
        sums = sb("sums", [P, 2, QB])
        weighted = sb("weighted", [P, QB])
        inv_total = sb("inv_total", [D, QB])
        x_res = sb("x_res", [D, 2, QB])
        result = sb("result", [D, 2, QB])
        part_max = sb("part_max", [P, 2, MAX_CHUNKS])
        neg_max = sb("neg_max", [P, 2])
        ident = sb("ident", [P, P])
        fold = sb("fold", [P, D])
        ones = sb("ones", [P, D])

        scores_ps = ps("scores_ps", [P, 2, 2, 512])
        out_ps = ps("out_ps", [P, 2, 512])
        ring_ps = ps("ring_ps", [P, 2, 512])

        loads = [sem(f"head{h}_loaded") for h in range(2)]
        const_loaded = sem("const_loaded")
        const_set = sem("const_set")
        x_loaded = [sem(f"x_res{r}_loaded") for r in range(2)]
        stored = [sem(f"result{r}_stored") for r in range(2)]
        scores_made = sem("scores_made")
        probs_made = sem("probs_made")
        hi_made = sem("p_hi_made")
        lo_made = sem("p_lo_made")
        summed = sem("summed")
        pv_made = sem("pv_made")
        ring_filled = sem("ring_filled")
        ring_read_v = sem("ring_read_by_vector")
        ring_read_s = sem("ring_read_by_scalar")
        max_made = sem("neg_max_made")
        chunk_read = sem("chunk_read")
        copied = sem("out_ps_copied")
        added = sem("added")

        def load_head(eng, h, pair):
            rows = slice(h * D, (h + 1) * D)
            done = loads[h]
            eng.dma_start(k_parts[h][0:D, :].bitcast(F32), k_hi_d[bass.ds(pair, 1), rows, :].rearrange("o p t -> (o p) t")).then_inc(done, 16)
            eng.dma_start(k_parts[h][D:P, :].bitcast(F32), k_lo_d[bass.ds(pair, 1), rows, :].rearrange("o p t -> (o p) t")).then_inc(done, 16)
            eng.dma_start(q_twice[h][0:D, 0:TP].bitcast(F32), q_hi_d[bass.ds(pair, 1), rows, :].rearrange("o p t -> (o p) t")).then_inc(done, 16)
            eng.dma_start(q_twice[h][D:P, 0:TP].bitcast(F32), q_hi_d[bass.ds(pair, 1), rows, :].rearrange("o p t -> (o p) t")).then_inc(done, 16)
            eng.dma_start(k_one[h][0:D, :].bitcast(F32), k_hi_d[bass.ds(pair, 1), rows, :].rearrange("o p t -> (o p) t")).then_inc(done, 16)
            eng.dma_start(q_max[h][0:D, 0:TP].bitcast(F32), q_lo_d[bass.ds(pair, 1), rows, :].rearrange("o p t -> (o p) t")).then_inc(done, 16)
            eng.dma_start(v_parts[h][:, :, :].bitcast(F32),
                          v_d[bass.ds(pair, 1), :, :, h * 2 * D:(h + 1) * 2 * D].rearrange("o k p n -> p (o k) n")
                          ).then_inc(done, 16)

        HEAD_LOADED = 16 * 7

        def tile_of(tile):
            return (tile // KT) % 2, tile % KT

        def ring_bank(n):
            return ring_ps[:, n % 2, :]

        def ring_matmul(pe, job, n):
            kind, which, part = job
            bank = ring_bank(n)
            if kind == "chunk":
                h, t = tile_of(which)
                k0 = part * QH
                width = min(QH, TP - k0)
                width = min(width, T - k0 + (T - k0) % 2)
                return nc.tensor.matmul(bank[:, 0:width], q_twice[h][:, t * P:(t + 1) * P],
                                        k_parts[h][:, k0:k0 + width], start=True, stop=True)
            if kind == "row":
                return nc.tensor.matmul(bank[D:D + 1, 0:P], neg_max[:, which % 2:which % 2 + 1],
                                        ident[:, :], start=True, stop=True)
            half = slice(part * QH, (part + 1) * QH)
            if kind == "total":
                return nc.tensor.matmul(bank[0:D, 0:QH], ones[:, :], sums[:, which % 2, half],
                                        start=True, stop=True)
            return nc.tensor.matmul(bank[0:D, 0:QH], fold[:, :], weighted[:, half],
                                    start=True, stop=True)

        def read_chunk(dve, tile, part, n):
            k0 = part * QH
            width = min(QH, T - k0)
            return nc.vector.reduce_max(part_max[:, tile % 2, part:part + 1], ring_bank(n)[:, 0:width], AX.X)

        def finish_tile(dve, tile):
            return nc.vector.tensor_reduce(neg_max[:, tile % 2:tile % 2 + 1], part_max[:, tile % 2, :],
                                           AX.X, ALU.max, negate=True)

        def write_row(act, tile, n):
            h, t = tile_of(tile)
            return nc.scalar.copy(q_max[h][D:D + 1, t * P:(t + 1) * P], ring_bank(n)[D:D + 1, 0:P])

        with nc.Block() as block:
            @block.sync
            def _(sp):
                sp.dma_start(ident[:, :], identity[:, :]).then_inc(const_loaded, 16)
                for half in range(2):
                    sp.dma_start(fold[half * D:(half + 1) * D, :], identity[0:D, 0:D]).then_inc(const_loaded, 16)
                load_head(sp, 0, 0)
                sp.wait_ge(const_loaded, 48)
                sp.wait_ge(loads[0], HEAD_LOADED)

            @block.gpsimd
            def _(pool):
                fills = [(ones[:, :], 1.0)]
                for h in range(2):
                    fills += [(k_one[h][D:D + 1, :].bitcast(F32), 1.0),
                              (q_twice[h][:, TP:TQ].bitcast(F32), 0.0),
                              (q_max[h][:, TP:TQ].bitcast(F32), 0.0)]
                for n, (where, value) in enumerate(fills):
                    if n >= 1:
                        pool.wait_ge(const_set, n)
                    nc.gpsimd.memset(where, value).then_inc(const_set, 1)

            @block.tensor
            def _(pe):
                pe.wait_ge(const_loaded, 48)
                pe.wait_ge(loads[0], HEAD_LOADED)
                n = 0
                for tile in range(FIRST_TILE):
                    for part in range(MAX_CHUNKS):
                        if n >= 2:
                            pe.wait_ge(chunk_read, n - 1 - tile)
                        if part < 2 and tile >= 1:
                            pe.wait_ge(ring_read_s, tile)
                        ring_matmul(pe, ("chunk", tile, part), n).then_inc(ring_filled, 1)
                        n += 1
                    pe.wait_ge(max_made, tile + 1)
                    pe.wait_ge(chunk_read, MAX_CHUNKS * (tile + 1))
                    ring_matmul(pe, ("row", tile, 0), n).then_inc(ring_filled, 1)
                    n += 1

            @block.vector
            def _(dve):
                n = 0
                for tile in range(FIRST_TILE):
                    if tile >= 2:
                        dve.wait_ge(ring_read_s, tile - 1)
                    for part in range(MAX_CHUNKS):
                        dve.wait_ge(ring_filled, n + 1)
                        read_chunk(dve, tile, part, n).then_inc(chunk_read, 1)
                        n += 1
                    n += 1
                    dve.wait_ge(chunk_read, MAX_CHUNKS * (tile + 1))
                    finish_tile(dve, tile).then_inc(max_made, 1)

            @block.scalar
            def _(act):
                for tile in range(FIRST_TILE):
                    n = (MAX_CHUNKS + 1) * tile + MAX_CHUNKS
                    act.wait_ge(ring_filled, n + 1)
                    write_row(act, tile, n).then_inc(ring_read_s, 1)

        clear_semaphores(nc, made)

        order, before_v, before_s = ring_positions(PLAN)

        def units_at(g, offset):
            unit, kt = divmod(g, KT)
            return unit - 1 if kt == offset and 1 <= unit <= 2 * UNITS else None

        with nc.Fori(0, PAIRS) as pair:
            with nc.Block() as block:
                def store(sp, u, pair):
                    h, j = divmod(u, UNITS)
                    q0, width = j * QB, min(QB, T - j * QB)
                    sp.wait_ge(added, u + 1)
                    sp.dma_start(out[bass.ds(pair, 1), h * D:(h + 1) * D, q0:q0 + width].rearrange("o p t -> (o p) t"),
                                 result[:, u % 2, 0:width]).then_inc(stored[u % 2], 16)

                @block.sync
                def _(sp):
                    load_head(sp, 1, pair)
                    for u in range(2 * UNITS):
                        h, j = divmod(u, UNITS)
                        q0, width = j * QB, min(QB, T - j * QB)
                        if u >= 2:
                            sp.wait_ge(added, u - 1)
                        sp.dma_start(x_res[:, u % 2, 0:width],
                                     x[bass.ds(pair, 1), h * D:(h + 1) * D, q0:q0 + width].rearrange("o p t -> (o p) t")
                                     ).then_inc(x_loaded[u % 2], 16)
                        if u == UNITS + 1:
                            sp.wait_ge(pv_made, HEAD_STEPS)
                            load_head(sp, 0, (pair + 1) & (PAIRS - 1))
                        if u >= 1:
                            store(sp, u - 1, pair)
                    store(sp, 2 * UNITS - 1, pair)
                    for r in range(2):
                        sp.wait_ge(stored[r], 16 * UNITS)
                    for h in range(2):
                        sp.wait_ge(loads[h], HEAD_LOADED)

                @block.tensor
                def _(pe):
                    n = 0
                    for g in range(STEPS + TAIL):
                        if g < STEPS:
                            unit, kt = divmod(g, KT)
                            h, j = divmod(unit, UNITS)
                            rows = keys_of(kt)
                            keys = slice(kt * P, kt * P + rows)
                            if g >= 2:
                                pe.wait_ge(probs_made, g - 1)
                            if kt == 0:
                                tiles = h * KT + min(KT, -(-(j + 1) * QB // P)) - FIRST_TILE
                                if tiles > 0:
                                    pe.wait_ge(ring_read_s, tiles)
                            for half in range(2):
                                q0 = j * QB + half * QH
                                nc.tensor.matmul(scores_ps[0:rows, g % 2, half, 0:QH], k_parts[h][:, keys],
                                                 q_twice[h][:, q0:q0 + QH], start=True, stop=False)
                            for half in range(2):
                                q0 = j * QB + half * QH
                                last = nc.tensor.matmul(scores_ps[0:rows, g % 2, half, 0:QH], k_one[h][:, keys],
                                                        q_max[h][:, q0:q0 + QH], start=False, stop=True)
                            last.then_inc(scores_made, 1)
                        for job in PLAN[g]:
                            kind, which, part = job
                            if n >= 2:
                                if order[n - 2][0] == "row":
                                    pe.wait_ge(ring_read_s, before_s[n - 1])
                                else:
                                    pe.wait_ge(ring_read_v, before_v[n - 1])
                            if kind == "chunk" and part == 0 and tile_of(which)[1] == 0:
                                pe.wait_ge(loads[tile_of(which)[0]], HEAD_LOADED)
                            if kind == "row":
                                pe.wait_ge(max_made, which - FIRST_TILE + 1)
                            if kind == "total" and part == 0:
                                pe.wait_ge(summed, (which + 1) * (KT - 1))
                            if kind == "output" and part == 0:
                                pe.wait_ge(copied, which + 1)
                            ring_matmul(pe, job, n).then_inc(ring_filled, 1)
                            n += 1
                        s = g - LAG
                        if 0 <= s < STEPS:
                            unit, kt = divmod(s, KT)
                            rows = keys_of(kt)
                            pe.wait_ge(lo_made, s + 1)
                            if kt == 0 and unit >= 1:
                                pe.wait_ge(copied, unit)
                            v_tile = v_parts[unit // UNITS][0:rows, kt, :]
                            for half in range(2):
                                cols = slice(half * QH, (half + 1) * QH)
                                nc.tensor.matmul(out_ps[:, half, 0:QH], v_tile, p_hi[0:rows, s % NHI, cols],
                                                 start=(kt == 0), stop=False)
                                last = nc.tensor.matmul(out_ps[:, half, 0:QH], v_tile, p_lo[0:rows, s % NLO, cols],
                                                        start=False, stop=(kt == KT - 1))
                            last.then_inc(pv_made, 1)

                @block.scalar
                def _(act):
                    n = 0
                    rows_due = []
                    for g in range(STEPS + TAIL):
                        if g < STEPS:
                            rows = keys_of(g % KT)
                            act.wait_ge(scores_made, g + 1)
                            if g >= NP:
                                act.wait_ge(lo_made, g - NP + 1)
                                act.wait_ge(summed, sums_through(g - NP))
                            nc.scalar.activation(
                                probs[0:rows, g % NP, :].rearrange("p (a n) -> p a n", a=2),
                                scores_ps[0:rows, g % 2, :, 0:QH], ACT.Exp, scale=float(D) ** 0.5
                            ).then_inc(probs_made, 1)
                        s = g - 1
                        if 0 <= s < STEPS:
                            rows = keys_of(s % KT)
                            act.wait_ge(probs_made, s + 1)
                            if s >= NHI:
                                act.wait_ge(pv_made, s - NHI + 1)
                            nc.scalar.copy(p_hi[0:rows, s % NHI, :], probs[0:rows, s % NP, :]).then_inc(hi_made, 1)
                        unit = units_at(g, LAG)
                        if unit is not None:
                            act.wait_ge(pv_made, (unit + 1) * KT)
                            if unit >= 1:
                                act.wait_ge(ring_filled, order.index(("output", unit - 1, 1)) + 1)
                            nc.scalar.copy(weighted[:, :].rearrange("p (a n) -> p a n", a=2),
                                           out_ps[:, :, 0:QH]).then_inc(copied, 1)
                        for kind, which, part in PLAN[g]:
                            if kind == "row":
                                act.wait_ge(ring_filled, n + 1)
                                write_row(act, which, n).then_inc(ring_read_s, 1)
                            n += 1

                @block.gpsimd
                def _(pool):
                    for g in range(STEPS):
                        rows = keys_of(g % KT)
                        pool.wait_ge(hi_made, g + 1)
                        if g >= NLO:
                            pool.wait_ge(pv_made, g - NLO + 1)
                        nc.gpsimd.tensor_tensor(p_lo[0:rows, g % NLO, :], probs[0:rows, g % NP, :],
                                                p_hi[0:rows, g % NHI, :].bitcast(F32),
                                                ALU.subtract).then_inc(lo_made, 1)

                @block.vector
                def _(dve):
                    n = 0
                    chunks = 0
                    adds = 0
                    for g in range(STEPS + TAIL):
                        for kind, which, part in PLAN[g]:
                            if kind == "row":
                                n += 1
                                continue
                            dve.wait_ge(ring_filled, n + 1)
                            half = slice(part * QH, (part + 1) * QH)
                            if kind == "chunk":
                                done = which - FIRST_TILE
                                if part == 0 and done >= 2:
                                    dve.wait_ge(ring_read_s, done - 1)
                                read_chunk(dve, which, part, n).then_inc(ring_read_v, 1)
                                if part == MAX_CHUNKS - 1:
                                    dve.wait_ge(ring_read_v, before_v[n + 1])
                                    finish_tile(dve, which).then_inc(max_made, 1)
                            elif kind == "total":
                                if which >= 1:
                                    dve.wait_ge(added, which)
                                nc.vector.reciprocal(inv_total[:, half], ring_bank(n)[0:D, 0:QH]).then_inc(ring_read_v, 1)
                            else:
                                r = which % 2
                                if which >= 2 and part == 0:
                                    dve.wait_ge(stored[r], 16 * (which // 2))
                                    dve.wait_ge(added, which - 1)
                                dve.wait_ge(ring_read_v, before_v[n])
                                nc.vector.tensor_tensor(result[:, r, half], ring_bank(n)[0:D, 0:QH],
                                                        inv_total[:, half], ALU.mult).then_inc(ring_read_v, 1)
                                if part == 1:
                                    j = which % UNITS
                                    width = min(QB, T - j * QB)
                                    dve.wait_ge(ring_read_v, before_v[n + 1])
                                    dve.wait_ge(x_loaded[r], 16 * (which // 2 + 1))
                                    nc.vector.tensor_tensor(result[:, r, 0:width], result[:, r, 0:width],
                                                            x_res[:, r, 0:width], ALU.add).then_inc(added, 1)
                            n += 1
                        s = g - 1
                        if 0 <= s < STEPS and s % KT > 0:
                            unit, kt = divmod(s, KT)
                            rows = keys_of(kt)
                            dve.wait_ge(probs_made, s + 1)
                            if kt == 1:
                                if unit >= 2:
                                    dve.wait_ge(ring_filled, order.index(("total", unit - 2, 1)) + 1)
                                first = probs[:, (s - 1) % NP, :]
                            else:
                                dve.wait_ge(summed, adds)
                                first = sums[:, unit % 2, :]
                            nc.vector.tensor_tensor(sums[0:rows, unit % 2, :], first[0:rows, :],
                                                    probs[0:rows, s % NP, :], ALU.add).then_inc(summed, 1)
                            adds += 1

            clear_semaphores(nc, made)


def attention_block(nc, x, w_t, pos_h_t, pos_w_t, group_mean, identity, out):
    q_hi_d = nc.dram_tensor("q_hi_d", [PAIRS, P, TP], F32, kind="Internal").ap()
    q_lo_d = nc.dram_tensor("q_lo_d", [PAIRS, P, TP], F32, kind="Internal").ap()
    k_hi_d = nc.dram_tensor("k_hi_d", [PAIRS, P, TP], F32, kind="Internal").ap()
    k_lo_d = nc.dram_tensor("k_lo_d", [PAIRS, P, TP], F32, kind="Internal").ap()
    v_d = nc.dram_tensor("v_d", [PAIRS, KT, P, 4 * D], F32, kind="Internal").ap()
    project(nc, x, w_t, pos_h_t, pos_w_t, group_mean, q_hi_d, q_lo_d, k_hi_d, k_lo_d, v_d)
    attend(nc, x, out, identity, q_hi_d, q_lo_d, k_hi_d, k_lo_d, v_d)


def kernel(**inputs):
    import concourse.bacc as bacc
    from concourse.bass_utils import run_bass_kernel_spmd

    x = np.ascontiguousarray(inputs["x"]).reshape(PAIRS, P, T)
    arrays = {
        "in_x": x,
        "in_w_t": np.ascontiguousarray(np.asarray(inputs["L0_conv_w_in"]).T),
        "in_pos_h_t": np.ascontiguousarray(np.asarray(inputs["L0_conv_pos_h"]).T),
        "in_pos_w_t": np.ascontiguousarray(np.asarray(inputs["L0_conv_pos_w"]).T),
        "in_group_mean": np.kron(np.eye(P // GROUP, dtype=np.float32),
                                 np.full((GROUP, GROUP), 1.0 / GROUP, np.float32)),
        "in_identity": np.eye(P, dtype=np.float32),
    }
    nc = bacc.Bacc("TRN2", target_bir_lowering=False, num_devices=1)
    args = [nc.dram_tensor(n, a.shape, F32, kind="ExternalInput").ap() for n, a in arrays.items()]
    out = nc.dram_tensor("out", [PAIRS, P, T], F32, kind="ExternalOutput").ap()
    attention_block(nc, *args, out)
    r = run_bass_kernel_spmd(nc, [arrays], core_ids=[0])
    return r.results[0]["out"].reshape(B, C, H, W)
```

```python
import concourse.bass as bass
from concourse import mybir
from contextlib import ExitStack
import numpy as np

B, C, H, W = 2, 512, 53, 53
HEADS = 8
D = C // HEADS
T = H * W
P = 128
CB = C // P
PAIRS = B * CB
GROUP = C // 32
GN_EPS = 1e-5

KT = -(-T // P)
TP = KT * P
LAST_KEYS = T - (KT - 1) * P
UNITS = 3
QH = 470
QB = 2 * QH
TQ = UNITS * QB

MAX_CHUNKS = -(-T // QH)
CHUNKS_A_STEP = MAX_CHUNKS // 3
LEAD = 27
LAG = 4
HI_LAG, LO_LAG = 1, 2

XC = 256
NXC = TP // XC
VT = XC // P

F32 = mybir.dt.float32
F32R = mybir.dt.float32r
ALU = mybir.AluOpType
ACT = mybir.ActivationFunctionType
AX = mybir.AxisListType


def clear_semaphores(nc, sems):
    for s in sems:
        nc.sync.sem_clear(s)
    nc.all_engine_barrier()


def project(nc, x, w_t, pos_h_t, pos_w_t, group_mean, q_hi_d, q_lo_d, k_hi_d, k_lo_d, v_d):
    with ExitStack() as ctx:
        def sb(name, shape, dt=F32):
            return ctx.enter_context(nc.sbuf_tensor(name, shape, dt))

        def ps(name, shape):
            return ctx.enter_context(nc.psum_tensor(name, shape, F32))

        made = []

        def sem(name):
            made.append(ctx.enter_context(nc.semaphore(name)))
            return made[-1]

        xs = sb("x_sb", [P, B, CB, TP])
        w32 = sb("w32", [P, 1, 3 * C])
        w_hi = sb("w_hi", [P, CB, 3 * C], F32R)
        w_lo = sb("w_lo", [P, CB, 3 * C], F32R)
        pos_h = sb("pos_h", [P, H])
        pos_w = sb("pos_w", [P, W])
        emb = sb("emb", [P, 1, TP])
        avg = sb("avg", [P, P])
        NST = -(-T // 512)
        stats = sb("stats", [P, B * CB, NST, 6])
        mv = sb("mv", [P, B * CB, 2])
        g_mean = sb("g_mean", [P, B * CB])
        dev = sb("dev", [P, B * CB])
        dev2 = sb("dev2", [P, B * CB])
        var_e = sb("var_e", [P, B * CB])
        std = sb("std", [P, B * CB])
        r0 = sb("r0", [P, B * CB])
        r1 = sb("r1", [P, B * CB])
        r2 = sb("r2", [P, B * CB])
        g_rstd = sb("g_rstd", [P, B * CB])
        mean_b = sb("mean_b", [P, CB])
        rstd_b = sb("rstd_b", [P, CB])
        xn = sb("xn", [P, CB, XC])
        xn_hi = sb("xn_hi", [P, 2, CB, XC], F32R)
        xn_lo = sb("xn_lo", [P, 2, CB, XC], F32R)
        q_hi = sb("q_hi", [P, CB, XC], F32R)
        q_lo = sb("q_lo", [P, CB, XC], F32R)
        k_sum = sb("k_sum", [P, CB, XC])
        k_hi = sb("k_hi", [P, CB, XC], F32R)
        k_lo = sb("k_lo", [P, CB, XC], F32R)
        v_parts = sb("v_parts", [P, VT, HEADS, 2, D], F32R)

        q_ps = ps("q_ps", [P, CB, XC])
        k_ps = ps("k_ps", [P, CB, XC])
        v_ps = ps("v_ps", [P, VT, C])
        stat_ps = ps("stat_ps", [P, 512])

        x_loaded = [sem(f"x{n}_loaded") for n in range(B * CB)]
        small_loaded = sem("small_loaded")
        w_loaded = sem("w_loaded")
        w_hi_ready = sem("w_hi_ready")
        w_lo_ready = sem("w_lo_ready")
        stat_ready = sem("stat_ready")
        stat_summed = sem("stat_summed")
        std_ready = sem("std_ready")
        chain = sem("dve_chain")

        with nc.Block() as block:
            @block.sync
            def _(sp):
                for b in range(B):
                    for c in range(CB):
                        sp.dma_start(xs[:, b, c, 0:T], x[b * CB + c, :, :]).then_inc(x_loaded[b * CB + c], 16)
                        if b == 0 and c == 0:
                            for half in range(2):
                                rows = slice(half * D, (half + 1) * D)
                                sp.dma_start(pos_h[rows, :], pos_h_t[:, :]).then_inc(small_loaded, 16)
                                sp.dma_start(pos_w[rows, :], pos_w_t[:, :]).then_inc(small_loaded, 16)
                            sp.dma_start(avg[:, :], group_mean[:, :]).then_inc(small_loaded, 16)

            @block.scalar
            def _(act):
                for c in range(CB):
                    if c:
                        act.wait_ge(w_lo_ready, c)
                    act.dma_start(w32[:, 0, :], w_t[c * P:(c + 1) * P, :]).then_inc(w_loaded, 16)
                    act.wait_ge(w_loaded, 16 * (c + 1))
                    nc.scalar.copy(w_hi[:, c, :], w32[:, 0, :]).then_inc(w_hi_ready, 1)
                act.wait_ge(stat_ready, 3)
                nc.scalar.activation(std[:, :], var_e[:, :], ACT.Sqrt).then_inc(std_ready, 1)

            @block.gpsimd
            def _(pool):
                nc.gpsimd.memset(xs[:, :, :, T:TP], 0.0)
                nc.gpsimd.memset(emb[:, :, T:TP], 0.0)
                for c in range(CB):
                    pool.wait_ge(w_hi_ready, c + 1)
                    nc.gpsimd.tensor_tensor(w_lo[:, c, :], w32[:, 0, :], w_hi[:, c, :].bitcast(F32),
                                            ALU.subtract).then_inc(w_lo_ready, 1)

            @block.tensor
            def _(pe):
                pe.wait_ge(small_loaded, 16 * 5)
                pe.wait_ge(stat_ready, 1)
                nc.tensor.matmul(stat_ps[:, 0:B * CB], avg[:, :], mv[:, :, 0],
                                 start=True, stop=True).then_inc(stat_summed, 1)
                pe.wait_ge(stat_ready, 2)
                nc.tensor.matmul(stat_ps[:, 0:B * CB], avg[:, :], dev2[:, :],
                                 start=True, stop=True).then_inc(stat_summed, 1)

            @block.vector
            def _(dve):
                links = [0]

                def link(ins):
                    links[0] += 1
                    ins.then_inc(chain, 1)
                    dve.wait_ge(chain, links[0])

                dve.wait_ge(small_loaded, 16 * 5)
                nc.vector.tensor_scalar(pos_h[:, :], pos_h[:, :], 1.0 / D, None, ALU.mult)
                link(nc.vector.tensor_scalar(pos_w[:, :], pos_w[:, :], 1.0 / D, None, ALU.mult))
                nc.vector.tensor_tensor(emb[:, 0, 0:T].rearrange("p (i j) -> p i j", j=W),
                                        pos_h[:, :].unsqueeze(2).broadcast_to([P, H, W]),
                                        pos_w[:, :].unsqueeze(1).broadcast_to([P, H, W]), ALU.add)
                for n in range(B * CB):
                    dve.wait_ge(x_loaded[n], 16)
                    for s in range(NST):
                        hi = min(T, (s + 1) * 512)
                        last = nc.vector.bn_stats(stats[:, n, s, :], xs[:, n // CB, n % CB, s * 512:hi])
                    link(last)
                    last = nc.vector.bn_aggr(mv[:, n, :], stats[:, n, :, :])
                last.then_inc(stat_ready, 1)
                dve.wait_ge(stat_summed, 1)
                link(nc.vector.tensor_copy(g_mean[:, :], stat_ps[:, 0:B * CB]))
                link(nc.vector.tensor_tensor(dev[:, :], mv[:, :, 0], g_mean[:, :], ALU.subtract))
                link(nc.vector.tensor_tensor(dev[:, :], dev[:, :], dev[:, :], ALU.mult))
                nc.vector.tensor_tensor(dev2[:, :], mv[:, :, 1], dev[:, :], ALU.add).then_inc(stat_ready, 1)
                dve.wait_ge(stat_summed, 2)
                nc.vector.tensor_scalar(var_e[:, :], stat_ps[:, 0:B * CB], GN_EPS, None,
                                        ALU.add).then_inc(stat_ready, 1)
                dve.wait_ge(std_ready, 1)
                link(nc.vector.reciprocal(r0[:, :], std[:, :]))
                link(nc.vector.tensor_tensor(r1[:, :], r0[:, :], r0[:, :], ALU.mult))
                link(nc.vector.tensor_tensor(r2[:, :], r1[:, :], var_e[:, :], ALU.mult))
                link(nc.vector.tensor_scalar(r1[:, :], r2[:, :], -0.5, 1.5, ALU.mult, ALU.add))
                nc.vector.tensor_tensor(g_rstd[:, :], r0[:, :], r1[:, :], ALU.mult)

        clear_semaphores(nc, made)

        ab_ready = sem("affine_ready")
        xn_ready = sem("xn_ready")
        xhi_ready = sem("xn_hi_ready")
        xlo_ready = sem("xn_lo_ready")
        q_made = sem("q_made")
        k_made = sem("k_made")
        v_made = sem("v_made")
        qhi_ready = sem("q_hi_ready")
        qlo_ready = sem("q_lo_ready")
        ksum_ready = sem("k_sum_ready")
        khi_ready = sem("k_hi_ready")
        klo_ready = sem("k_lo_ready")
        vhi_ready = sem("v_hi_ready")
        vlo_ready = sem("v_lo_ready")
        q_stored = sem("q_stored")
        k_stored = sem("k_stored")
        v_stored = sem("v_stored")
        loop_sems = made[-18:]

        with nc.Fori(0, B) as b:
            with nc.Block() as block:
                @block.sync
                def _(sp):
                    for i in range(NXC):
                        at = slice(i * XC, (i + 1) * XC)
                        sp.wait_ge(qlo_ready, i + 1)
                        sp.dma_start(q_hi_d[bass.ds(b * CB, CB), :, at].rearrange("m p t -> p m t"),
                                     q_hi[:, :, :].bitcast(F32)).then_inc(q_stored, 16)
                        sp.dma_start(q_lo_d[bass.ds(b * CB, CB), :, at].rearrange("m p t -> p m t"),
                                     q_lo[:, :, :].bitcast(F32)).then_inc(q_stored, 16)
                        sp.wait_ge(klo_ready, i + 1)
                        sp.dma_start(k_hi_d[bass.ds(b * CB, CB), :, at].rearrange("m p t -> p m t"),
                                     k_hi[:, :, :].bitcast(F32)).then_inc(k_stored, 16)
                        sp.dma_start(k_lo_d[bass.ds(b * CB, CB), :, at].rearrange("m p t -> p m t"),
                                     k_lo[:, :, :].bitcast(F32)).then_inc(k_stored, 16)
                        sp.wait_ge(vlo_ready, i + 1)
                        for t in range(VT):
                            sp.dma_start(v_d[bass.ds(b * CB, CB), i * VT + t, :, :].rearrange("m p n -> p m n"),
                                         v_parts[:, t, :, :, :].bitcast(F32).rearrange("p (m h) s d -> p m (h s d)", m=CB)
                                         ).then_inc(v_stored, 16)
                    sp.wait_ge(q_stored, 32 * NXC)
                    sp.wait_ge(k_stored, 32 * NXC)
                    sp.wait_ge(v_stored, 16 * VT * NXC)

                @block.vector
                def _(dve):
                    nc.vector.tensor_copy(mean_b[:, :], g_mean[:, bass.ds(b * CB, CB)]).then_inc(ab_ready, 1)
                    nc.vector.tensor_copy(rstd_b[:, :], g_rstd[:, bass.ds(b * CB, CB)]).then_inc(ab_ready, 1)
                    dve.wait_ge(ab_ready, 2)

                    def normalise(i):
                        if i >= 1:
                            dve.wait_ge(xlo_ready, i)
                        for c in range(CB):
                            last = nc.vector.tensor_scalar(
                                xn[:, c, :], xs[:, bass.ds(b, 1), c, i * XC:(i + 1) * XC],
                                mean_b[:, c:c + 1], rstd_b[:, c:c + 1], ALU.subtract, ALU.mult)
                        last.then_inc(xn_ready, 1)
                        dve.wait_ge(xhi_ready, i + 1)
                        nc.vector.tensor_tensor(xn_lo[:, i % 2, :, :], xn[:, :, :],
                                                xn_hi[:, i % 2, :, :].bitcast(F32),
                                                ALU.subtract).then_inc(xlo_ready, 1)

                    normalise(0)
                    for i in range(NXC):
                        if i + 1 < NXC:
                            if i >= 1:
                                dve.wait_ge(v_made, i)
                            normalise(i + 1)
                        dve.wait_ge(qhi_ready, i + 1)
                        nc.vector.tensor_tensor(q_lo[:, :, :], q_ps[:, :, :], q_hi[:, :, :].bitcast(F32),
                                                ALU.subtract).then_inc(qlo_ready, 1)
                        dve.wait_ge(k_made, i + 1)
                        if i >= 1:
                            dve.wait_ge(klo_ready, i)
                        nc.vector.tensor_tensor(
                            k_sum[:, :, :], k_ps[:, :, :],
                            emb[:, :, i * XC:(i + 1) * XC].broadcast_to([P, CB, XC]),
                            ALU.add).then_inc(ksum_ready, 1)
                        dve.wait_ge(vhi_ready, i + 1)
                        nc.vector.tensor_tensor(
                            v_parts[:, :, :, 1, :],
                            v_ps[:, :, :].rearrange("p t (h d) -> p t h d", d=D),
                            v_parts[:, :, :, 0, :].bitcast(F32), ALU.subtract).then_inc(vlo_ready, 1)

                @block.scalar
                def _(act):
                    def round_x(i):
                        act.wait_ge(xn_ready, i + 1)
                        nc.scalar.copy(xn_hi[:, i % 2, :, :], xn[:, :, :]).then_inc(xhi_ready, 1)

                    round_x(0)
                    for i in range(NXC):
                        if i + 1 < NXC:
                            round_x(i + 1)
                        act.wait_ge(q_made, i + 1)
                        if i >= 1:
                            act.wait_ge(q_stored, 32 * i)
                        nc.scalar.copy(q_hi[:, :, :], q_ps[:, :, :]).then_inc(qhi_ready, 1)
                        act.wait_ge(ksum_ready, i + 1)
                        if i >= 1:
                            act.wait_ge(k_stored, 32 * i)
                        nc.scalar.copy(k_hi[:, :, :], k_sum[:, :, :]).then_inc(khi_ready, 1)
                        act.wait_ge(v_made, i + 1)
                        if i >= 1:
                            act.wait_ge(v_stored, 16 * VT * i)
                        nc.scalar.copy(v_parts[:, :, :, 0, :],
                                       v_ps[:, :, :].rearrange("p t (h d) -> p t h d", d=D)
                                       ).then_inc(vhi_ready, 1)

                @block.gpsimd
                def _(pool):
                    for i in range(NXC):
                        pool.wait_ge(khi_ready, i + 1)
                        nc.gpsimd.tensor_tensor(k_lo[:, :, :], k_sum[:, :, :], k_hi[:, :, :].bitcast(F32),
                                                ALU.subtract).then_inc(klo_ready, 1)

                @block.tensor
                def _(pe):
                    terms = [(c, w, xp) for c in range(CB)
                             for w, xp in ((w_hi, xn_hi), (w_lo, xn_hi), (w_hi, xn_lo))]

                    def channels(out, o0, i):
                        for n, (c, w, xp) in enumerate(terms):
                            last = nc.tensor.matmul(out, w[:, c, o0:o0 + P], xp[:, i % 2, c, :],
                                                    start=(n == 0), stop=(n == len(terms) - 1))
                        return last

                    for i in range(NXC):
                        pe.wait_ge(xlo_ready, i + 1)
                        if i >= 1:
                            pe.wait_ge(qlo_ready, i)
                        for m in range(CB):
                            last = channels(q_ps[:, m, :], m * P, i)
                        last.then_inc(q_made, 1)
                        if i >= 1:
                            pe.wait_ge(ksum_ready, i)
                        for m in range(CB):
                            last = channels(k_ps[:, m, :], C + m * P, i)
                        last.then_inc(k_made, 1)
                        if i >= 1:
                            pe.wait_ge(vlo_ready, i)
                        for t in range(VT):
                            for n, (c, w, xp) in enumerate(terms):
                                last = nc.tensor.matmul(v_ps[:, t, :], xp[:, i % 2, c, t * P:(t + 1) * P],
                                                        w[:, c, 2 * C:3 * C],
                                                        start=(n == 0), stop=(n == len(terms) - 1))
                        last.then_inc(v_made, 1)

            clear_semaphores(nc, loop_sems)



HEAD_STEPS = UNITS * KT
STEPS = 2 * HEAD_STEPS
PAIR_UNITS = 2 * UNITS
FIRST_TILE = LEAD // 3
START = 8
NP, NHI, NLO = 4, 6, 4
TOTAL_AT, SPREAD_AT, OUTPUT_AT = 3, 4, 6
Q_TILES = [(half, q0, min(P, QH - q0)) for half in range(2) for q0 in range(0, QH, P)]


def keys_of(kt):
    return LAST_KEYS if kt == KT - 1 else P


def sums_through(g):
    unit, kt = divmod(g, KT)
    return unit * (KT - 1) + max(kt, 1)


def sums_before(g):
    unit, kt = divmod(g, KT)
    return unit * (KT - 1) + max(kt - 1, 0)


def ring_jobs(g):
    tile, third = divmod(g + LEAD, 3)
    unit, kt = divmod(g, KT)
    chunks = [("chunk", tile, CHUNKS_A_STEP * third + n) for n in range(CHUNKS_A_STEP)]
    others = []
    if third == 1 and tile - 1 >= FIRST_TILE:
        others.append(("row", tile - 1, 0))
    for kind, at in (("total", TOTAL_AT), ("spread", SPREAD_AT), ("output", OUTPUT_AT)):
        if unit >= 1 and kt == at:
            others.append((kind, unit - 1, 0))
    return [chunks[0], *others, *chunks[1:]]


class Ring:
    SCALAR = ("row", "spread")

    def __init__(self, steps):
        self.jobs = [job for g in steps for job in ring_jobs(g)]
        self.scalar = [0]
        for kind, _, _ in self.jobs:
            self.scalar.append(self.scalar[-1] + (kind in self.SCALAR))
        self.first = {g: sum(len(ring_jobs(s)) for s in steps if s < g) for g in steps}

    def numbered(self, g):
        return [(self.first[g] + n, *job) for n, job in enumerate(ring_jobs(g))]

    def by_scalar(self, n):
        return self.jobs[n][0] in self.SCALAR

    def read_by_scalar(self, n):
        return self.scalar[n + 1]

    def read_by_vector(self, n):
        return n + 1 - self.scalar[n + 1]

    def find(self, *job):
        return self.jobs.index(job) if job in self.jobs else None


def attend(nc, x, out, identity, q_hi_d, q_lo_d, k_hi_d, k_lo_d, v_d):
    with ExitStack() as ctx:
        def sb(name, shape, dt=F32):
            return ctx.enter_context(nc.sbuf_tensor(name, shape, dt))

        def ps(name, shape):
            return ctx.enter_context(nc.psum_tensor(name, shape, F32))

        made = []

        def sem(name):
            made.append(ctx.enter_context(nc.semaphore(name)))
            return made[-1]

        k_parts = [sb(f"k_parts{h}", [P, TP], F32R) for h in range(2)]
        k_one = [sb(f"k_one{h}", [D + 1, TP], F32R) for h in range(2)]
        q_twice = [sb(f"q_twice{h}", [P, TQ], F32R) for h in range(2)]
        q_max = [sb(f"q_max{h}", [D + 1, TQ], F32R) for h in range(2)]
        v_parts = [sb(f"v_parts{h}", [P, KT, 2 * D], F32R) for h in range(2)]
        probs = sb("probs", [P, NP, QB])
        p_hi = sb("p_hi", [P, NHI, QB], F32R)
        p_lo = sb("p_lo", [P, NLO, QB], F32R)
        sums = sb("sums", [P, 2, QB])
        weighted = sb("weighted", [P, QB])
        inv_cols = sb("inv_cols", [P, len(Q_TILES)])
        inv_total = sb("inv_total", [P, QH])
        x_res = sb("x_res", [P, 2, QH])
        result = sb("result", [P, 2, QH])
        part_max = sb("part_max", [P, 2, MAX_CHUNKS])
        neg_max = sb("neg_max", [P, 2])
        ident = sb("ident", [P, P])
        fold = sb("fold", [P, D])
        ones = sb("ones", [P, 1])

        scores_ps = ps("scores_ps", [P, 2, 2, 512])
        out_ps = ps("out_ps", [P, 2, 512])
        ring_ps = ps("ring_ps", [P, 2, 512])

        loads = [sem(f"head{h}_loaded") for h in range(2)]
        const_loaded = sem("const_loaded")
        const_set = sem("const_set")
        x_loaded = [sem(f"x_res{r}_loaded") for r in range(2)]
        stored = [sem(f"result{r}_stored") for r in range(2)]
        scores_made = sem("scores_made")
        probs_made = sem("probs_made")
        hi_made = sem("p_hi_made")
        lo_made = sem("p_lo_made")
        summed = sem("summed")
        pv_made = sem("pv_made")
        ring_filled = sem("ring_filled")
        ring_read_v = sem("ring_read_by_vector")
        ring_read_s = sem("ring_read_by_scalar")
        max_made = sem("neg_max_made")
        chunk_read = sem("chunk_read")
        copied = sem("out_ps_copied")
        added = sem("added")

        def load_head(eng, h, pair):
            rows = slice(h * D, (h + 1) * D)
            for where, what in ((k_parts[h][0:D, :], k_hi_d), (k_parts[h][D:P, :], k_lo_d),
                                (q_twice[h][0:D, 0:TP], q_hi_d), (q_twice[h][D:P, 0:TP], q_hi_d),
                                (k_one[h][0:D, :], k_hi_d), (q_max[h][0:D, 0:TP], q_lo_d)):
                eng.dma_start(where.bitcast(F32),
                              what[bass.ds(pair, 1), rows, :].rearrange("o p t -> (o p) t")
                              ).then_inc(loads[h], 16)
            eng.dma_start(v_parts[h][:, :, :].bitcast(F32),
                          v_d[bass.ds(pair, 1), :, :, h * 2 * D:(h + 1) * 2 * D].rearrange("o k p n -> p (o k) n")
                          ).then_inc(loads[h], 16)

        HEAD_LOADED = 16 * 7

        def tile_of(tile):
            return (tile // KT) % 2, tile % KT

        def block_of(unit):
            return (unit // UNITS) % 2, (unit % UNITS) * QB

        def half_widths(unit):
            q0 = block_of(unit)[1]
            return [(q0 + half * QH, min(QH, T - q0 - half * QH)) for half in range(2)]

        def ring_bank(n):
            return ring_ps[:, n % 2, :]

        def fill_bank(pe, n, kind, which):
            bank = ring_bank(n)
            if kind == "row":
                return nc.tensor.matmul(bank[D:D + 1, 0:P], neg_max[:, which % 2:which % 2 + 1],
                                        ident[:, :], start=True, stop=True)
            if kind == "total":
                for n, (half, q0, width) in enumerate(Q_TILES):
                    at = half * QH + q0
                    last = nc.tensor.matmul(bank[0:width, n:n + 1], sums[:, which % 2, at:at + width],
                                            ones[:, :], start=True, stop=True)
            elif kind == "spread":
                for n, (half, q0, width) in enumerate(Q_TILES):
                    last = nc.tensor.matmul(bank[half * D:(half + 1) * D, q0:q0 + width],
                                            inv_cols[0:width, n:n + 1].broadcast_to([width, D]),
                                            ident[0:width, 0:width], start=True, stop=True)
            else:
                for half in range(2):
                    last = nc.tensor.matmul(bank[half * D:(half + 1) * D, 0:QH], fold[:, :],
                                            weighted[:, half * QH:(half + 1) * QH], start=True, stop=True)
            return last

        def fill_chunk(pe, n, tile, part):
            h, t = tile_of(tile)
            k0 = part * QH
            width = min(QH, T - k0 + (T - k0) % 2)
            return nc.tensor.matmul(ring_bank(n)[:, 0:width], q_twice[h][:, t * P:(t + 1) * P],
                                    k_parts[h][:, k0:k0 + width], start=True, stop=True)

        def read_chunk(dve, n, tile, part):
            width = min(QH, T - part * QH)
            return nc.vector.reduce_max(part_max[:, tile % 2, part:part + 1], ring_bank(n)[:, 0:width], AX.X)

        def finish_tile(dve, tile):
            return nc.vector.tensor_reduce(neg_max[:, tile % 2:tile % 2 + 1], part_max[:, tile % 2, :],
                                           AX.X, ALU.max, negate=True)

        def write_row(act, n, tile):
            h, t = tile_of(tile)
            return nc.scalar.copy(q_max[h][D:D + 1, t * P:(t + 1) * P], ring_bank(n)[D:D + 1, 0:P])

        with nc.Block() as block:
            @block.sync
            def _(sp):
                sp.dma_start(ident[:, :], identity[:, :]).then_inc(const_loaded, 16)
                for half in range(2):
                    sp.dma_start(fold[half * D:(half + 1) * D, :], identity[0:D, 0:D]).then_inc(const_loaded, 16)
                load_head(sp, 0, 0)
                sp.wait_ge(const_loaded, 48)
                sp.wait_ge(loads[0], HEAD_LOADED)

            @block.gpsimd
            def _(pool):
                fills = [(ones[:, :], 1.0), (x_res[:, :, :], 0.0)]
                for h in range(2):
                    fills += [(k_one[h][D:D + 1, :].bitcast(F32), 1.0),
                              (q_twice[h][:, TP:TQ].bitcast(F32), 0.0),
                              (q_max[h][:, TP:TQ].bitcast(F32), 0.0)]
                for n, (where, value) in enumerate(fills):
                    if n >= 1:
                        pool.wait_ge(const_set, n)
                    nc.gpsimd.memset(where, value).then_inc(const_set, 1)

            @block.tensor
            def _(pe):
                pe.wait_ge(const_loaded, 48)
                pe.wait_ge(loads[0], HEAD_LOADED)
                n = 0
                for tile in range(FIRST_TILE):
                    for part in range(MAX_CHUNKS):
                        if n >= 2:
                            pe.wait_ge(chunk_read, n - 1 - tile)
                        if part < 2 and tile >= 1:
                            pe.wait_ge(ring_read_s, tile)
                        fill_chunk(pe, n, tile, part).then_inc(ring_filled, 1)
                        n += 1
                    pe.wait_ge(max_made, tile + 1)
                    pe.wait_ge(chunk_read, MAX_CHUNKS * (tile + 1))
                    fill_bank(pe, n, "row", tile).then_inc(ring_filled, 1)
                    n += 1

            @block.vector
            def _(dve):
                n = 0
                for tile in range(FIRST_TILE):
                    if tile >= 2:
                        dve.wait_ge(ring_read_s, tile - 1)
                    for part in range(MAX_CHUNKS):
                        dve.wait_ge(ring_filled, n + 1)
                        read_chunk(dve, n, tile, part).then_inc(chunk_read, 1)
                        n += 1
                    n += 1
                    dve.wait_ge(chunk_read, MAX_CHUNKS * (tile + 1))
                    finish_tile(dve, tile).then_inc(max_made, 1)

            @block.scalar
            def _(act):
                for tile in range(FIRST_TILE):
                    n = (MAX_CHUNKS + 1) * tile + MAX_CHUNKS
                    act.wait_ge(ring_filled, n + 1)
                    write_row(act, n, tile).then_inc(ring_read_s, 1)

        clear_semaphores(nc, made)

        def run_steps(block, begin, end):
            steps = range(begin, end)
            ring = Ring(steps)
            probs_before = begin
            lo_before = max(0, begin - LO_LAG)
            summed_before = sums_before(max(0, begin - LO_LAG))
            pv_before = max(0, begin - LAG)
            tiles_before = (begin + LEAD) // 3

            def multiply_v(pe, s):
                if s < 0:
                    return
                unit, kt = divmod(s, KT)
                rows = keys_of(kt)
                if s >= lo_before:
                    pe.wait_ge(lo_made, s + 1 - lo_before)
                if kt == 0 and unit >= 1:
                    pe.wait_ge(copied, unit)
                v_tile = v_parts[block_of(unit)[0]][0:rows, kt, :]
                for half in range(2):
                    cols = slice(half * QH, (half + 1) * QH)
                    nc.tensor.matmul(out_ps[:, half, 0:QH], v_tile, p_hi[0:rows, s % NHI, cols],
                                     start=(kt == 0), stop=False)
                    last = nc.tensor.matmul(out_ps[:, half, 0:QH], v_tile, p_lo[0:rows, s % NLO, cols],
                                            start=False, stop=(kt == KT - 1))
                last.then_inc(pv_made, 1)

            @block.tensor
            def _(pe):
                for g in steps:
                    unit, kt = divmod(g, KT)
                    h, q0 = block_of(unit)
                    rows = keys_of(kt)
                    keys = slice(kt * P, kt * P + rows)
                    if g - 1 > probs_before:
                        pe.wait_ge(probs_made, g - 1 - probs_before)
                    if kt == 0:
                        tile = unit // UNITS * KT + min(KT, -(-(q0 + QB) // P)) - 1
                        n = ring.find("row", tile, 0)
                        if n is not None:
                            pe.wait_ge(ring_read_s, ring.read_by_scalar(n))
                    for half in range(2):
                        at = q0 + half * QH
                        nc.tensor.matmul(scores_ps[0:rows, g % 2, half, 0:QH], k_parts[h][:, keys],
                                         q_twice[h][:, at:at + QH], start=True, stop=False)
                    for half in range(2):
                        at = q0 + half * QH
                        last = nc.tensor.matmul(scores_ps[0:rows, g % 2, half, 0:QH], k_one[h][:, keys],
                                                q_max[h][:, at:at + QH], start=False, stop=True)
                    last.then_inc(scores_made, 1)
                    for place, (n, kind, which, part) in enumerate(ring.numbered(g)):
                        if place == 1:
                            multiply_v(pe, g - LAG)
                        if n >= 2 and ring.by_scalar(n - 2):
                            pe.wait_ge(ring_read_s, ring.read_by_scalar(n - 2))
                        if n >= 2 and not ring.by_scalar(n - 2):
                            pe.wait_ge(ring_read_v, ring.read_by_vector(n - 2))
                        if kind == "chunk":
                            if part == 0 and tile_of(which)[1] == 0:
                                pe.wait_ge(loads[tile_of(which)[0]], HEAD_LOADED)
                            fill_chunk(pe, n, which, part).then_inc(ring_filled, 1)
                            continue
                        if kind == "row" and which >= tiles_before:
                            pe.wait_ge(max_made, which + 1 - tiles_before)
                        if kind == "total":
                            pe.wait_ge(summed, (which + 1) * (KT - 1) - summed_before)
                        if kind == "spread":
                            pe.wait_ge(ring_read_v, ring.read_by_vector(ring.find("total", which, 0)))
                        if kind == "output":
                            pe.wait_ge(copied, which + 1)
                        fill_bank(pe, n, kind, which).then_inc(ring_filled, 1)

            @block.scalar
            def _(act):
                for g in steps:
                    unit, kt = divmod(g, KT)
                    if kt == LAG and unit >= 1:
                        act.wait_ge(pv_made, unit * KT - pv_before)
                        if unit >= 2:
                            act.wait_ge(ring_filled, ring.find("output", unit - 2, 0) + 1)
                        nc.scalar.copy(weighted[:, :].rearrange("p (a n) -> p a n", a=2),
                                       out_ps[:, :, 0:QH]).then_inc(copied, 1)
                    rows = keys_of(kt)
                    act.wait_ge(scores_made, g + 1 - begin)
                    if g - NP >= lo_before:
                        act.wait_ge(lo_made, g - NP + 1 - lo_before)
                    if g >= NP and sums_through(g - NP) > summed_before:
                        act.wait_ge(summed, sums_through(g - NP) - summed_before)
                    nc.scalar.activation(
                        probs[0:rows, g % NP, :].rearrange("p (a n) -> p a n", a=2),
                        scores_ps[0:rows, g % 2, :, 0:QH], ACT.Exp, scale=float(D) ** 0.5
                    ).then_inc(probs_made, 1)
                    s = g - HI_LAG
                    if s >= 0:
                        rows = keys_of(s % KT)
                        if s >= probs_before:
                            act.wait_ge(probs_made, s + 1 - probs_before)
                        if s - NHI >= pv_before:
                            act.wait_ge(pv_made, s - NHI + 1 - pv_before)
                        nc.scalar.copy(p_hi[0:rows, s % NHI, :], probs[0:rows, s % NP, :]).then_inc(hi_made, 1)
                    for n, kind, which, part in ring.numbered(g):
                        if ring.by_scalar(n):
                            act.wait_ge(ring_filled, n + 1)
                        if kind == "row":
                            write_row(act, n, which).then_inc(ring_read_s, 1)
                        if kind == "spread":
                            if which >= 1:
                                act.wait_ge(ring_read_v, ring.read_by_vector(ring.find("output", which - 1, 0)))
                            nc.scalar.copy(inv_total[:, :], ring_bank(n)[:, 0:QH]).then_inc(ring_read_s, 1)

            @block.gpsimd
            def _(pool):
                for s in range(max(0, begin - LO_LAG), end - LO_LAG):
                    rows = keys_of(s % KT)
                    if s >= max(0, begin - HI_LAG):
                        pool.wait_ge(hi_made, s + 1 - max(0, begin - HI_LAG))
                    if s - NLO >= pv_before:
                        pool.wait_ge(pv_made, s - NLO + 1 - pv_before)
                    nc.gpsimd.tensor_tensor(p_lo[0:rows, s % NLO, :], probs[0:rows, s % NP, :],
                                            p_hi[0:rows, s % NHI, :].bitcast(F32),
                                            ALU.subtract).then_inc(lo_made, 1)

            @block.vector
            def _(dve):
                def add_sums(s):
                    unit, kt = divmod(s, KT)
                    if s < 0 or kt == 0:
                        return
                    rows = keys_of(kt)
                    if s >= probs_before:
                        dve.wait_ge(probs_made, s + 1 - probs_before)
                    first = sums[:, unit % 2, :]
                    if kt == 1:
                        n = ring.find("total", unit - 2, 0)
                        if n is not None:
                            dve.wait_ge(ring_filled, n + 1)
                        first = probs[:, (s - 1) % NP, :]
                    elif sums_before(s) > summed_before:
                        dve.wait_ge(summed, sums_before(s) - summed_before)
                    nc.vector.tensor_tensor(sums[0:rows, unit % 2, :], first[0:rows, :],
                                            probs[0:rows, s % NP, :], ALU.add).then_inc(summed, 1)

                for g in steps:
                    for place, (n, kind, which, part) in enumerate(ring.numbered(g)):
                        if place == 1:
                            add_sums(g - LO_LAG)
                        if ring.by_scalar(n):
                            continue
                        dve.wait_ge(ring_filled, n + 1)
                        if kind == "chunk":
                            row = ring.find("row", which - 2, 0)
                            if part == 0 and row is not None:
                                dve.wait_ge(ring_read_s, ring.read_by_scalar(row))
                            read_chunk(dve, n, which, part).then_inc(ring_read_v, 1)
                            if part == MAX_CHUNKS - 1:
                                dve.wait_ge(ring_read_v, ring.read_by_vector(n))
                                finish_tile(dve, which).then_inc(max_made, 1)
                        elif kind == "total":
                            nc.vector.reciprocal(inv_cols[:, :], ring_bank(n)[:, 0:len(Q_TILES)]).then_inc(ring_read_v, 1)
                        else:
                            r = which % 2
                            if which >= 2:
                                dve.wait_ge(stored[r], 32 * (which // 2))
                                dve.wait_ge(added, which - 1)
                            spread = ring.find("spread", which, 0)
                            dve.wait_ge(ring_read_s, ring.read_by_scalar(spread))
                            nc.vector.tensor_tensor(result[:, r, :], ring_bank(n)[:, 0:QH],
                                                    inv_total[:, :], ALU.mult).then_inc(ring_read_v, 1)
                            dve.wait_ge(ring_read_v, ring.read_by_vector(n))
                            dve.wait_ge(x_loaded[r], 32 * (which // 2 + 1))
                            nc.vector.tensor_tensor(result[:, r, :], result[:, r, :],
                                                    x_res[:, r, :], ALU.add).then_inc(added, 1)

        with nc.Block() as block:
            run_steps(block, 0, START)

        clear_semaphores(nc, made)

        with nc.Fori(0, PAIRS) as pair:
            with nc.Block() as block:
                run_steps(block, START, START + STEPS)

                @block.sync
                def _(sp):
                    load_head(sp, 1, pair)
                    for u in range(PAIR_UNITS + 1):
                        if u < PAIR_UNITS:
                            if u >= 2:
                                sp.wait_ge(added, u - 1)
                            h = block_of(u)[0]
                            for half, (q, width) in enumerate(half_widths(u)):
                                sp.dma_start(x_res[half * D:(half + 1) * D, u % 2, 0:width],
                                             x[bass.ds(pair, 1), h * D:(h + 1) * D, q:q + width]
                                             .rearrange("o p t -> (o p) t")).then_inc(x_loaded[u % 2], 16)
                        if u == UNITS + 1:
                            sp.wait_ge(pv_made, HEAD_STEPS - (START - LAG))
                            load_head(sp, 0, (pair + 1) & (PAIRS - 1))
                        if u >= 1:
                            h = block_of(u - 1)[0]
                            sp.wait_ge(added, u)
                            for half, (q, width) in enumerate(half_widths(u - 1)):
                                sp.dma_start(out[bass.ds(pair, 1), h * D:(h + 1) * D, q:q + width]
                                             .rearrange("o p t -> (o p) t"),
                                             result[half * D:(half + 1) * D, (u - 1) % 2, 0:width]
                                             ).then_inc(stored[(u - 1) % 2], 16)
                    for r in range(2):
                        sp.wait_ge(stored[r], 32 * UNITS)
                    for h in range(2):
                        sp.wait_ge(loads[h], HEAD_LOADED)

            clear_semaphores(nc, made)


def attention_block(nc, x, w_t, pos_h_t, pos_w_t, group_mean, identity, out):
    q_hi_d = nc.dram_tensor("q_hi_d", [PAIRS, P, TP], F32, kind="Internal").ap()
    q_lo_d = nc.dram_tensor("q_lo_d", [PAIRS, P, TP], F32, kind="Internal").ap()
    k_hi_d = nc.dram_tensor("k_hi_d", [PAIRS, P, TP], F32, kind="Internal").ap()
    k_lo_d = nc.dram_tensor("k_lo_d", [PAIRS, P, TP], F32, kind="Internal").ap()
    v_d = nc.dram_tensor("v_d", [PAIRS, KT, P, 4 * D], F32, kind="Internal").ap()
    project(nc, x, w_t, pos_h_t, pos_w_t, group_mean, q_hi_d, q_lo_d, k_hi_d, k_lo_d, v_d)
    attend(nc, x, out, identity, q_hi_d, q_lo_d, k_hi_d, k_lo_d, v_d)


def kernel(**inputs):
    import concourse.bacc as bacc
    from concourse.bass_utils import run_bass_kernel_spmd

    x = np.ascontiguousarray(inputs["x"]).reshape(PAIRS, P, T)
    arrays = {
        "in_x": x,
        "in_w_t": np.ascontiguousarray(np.asarray(inputs["L0_conv_w_in"]).T),
        "in_pos_h_t": np.ascontiguousarray(np.asarray(inputs["L0_conv_pos_h"]).T),
        "in_pos_w_t": np.ascontiguousarray(np.asarray(inputs["L0_conv_pos_w"]).T),
        "in_group_mean": np.kron(np.eye(P // GROUP, dtype=np.float32),
                                 np.full((GROUP, GROUP), 1.0 / GROUP, np.float32)),
        "in_identity": np.eye(P, dtype=np.float32),
    }
    nc = bacc.Bacc("TRN2", target_bir_lowering=False, num_devices=1)
    args = [nc.dram_tensor(n, a.shape, F32, kind="ExternalInput").ap() for n, a in arrays.items()]
    out = nc.dram_tensor("out", [PAIRS, P, T], F32, kind="ExternalOutput").ap()
    attention_block(nc, *args, out)
    r = run_bass_kernel_spmd(nc, [arrays], core_ids=[0])
    return r.results[0]["out"].reshape(B, C, H, W)
```

```python
import concourse.bass as bass
from concourse import mybir
from contextlib import ExitStack
import numpy as np

B, C, H, W = 2, 512, 53, 53
HEADS = 8
D = C // HEADS
T = H * W
P = 128
CB = C // P
PAIRS = B * CB
GROUP = C // 32
GN_EPS = 1e-5

KT = -(-T // P)
TP = KT * P
LAST_KEYS = T - (KT - 1) * P
UNITS = 6
QB = 470
TQ = UNITS * QB
UNIT_STEPS = KT // 2
HEAD_STEPS = UNITS * UNIT_STEPS
STEPS = 2 * HEAD_STEPS
PAIR_UNITS = 2 * UNITS
DUO = 2 * UNIT_STEPS
DUOS = UNITS

MAX_CHUNKS = -(-T // QB)
TILE_STEPS = HEAD_STEPS // KT
CHUNKS_A_STEP = MAX_CHUNKS // TILE_STEPS
LEAD = 17
HI_LAG, LO_LAG, LAG = 1, 2, 5

XC = 256
NXC = TP // XC
VT = XC // P

F32 = mybir.dt.float32
F32R = mybir.dt.float32r
ALU = mybir.AluOpType
ACT = mybir.ActivationFunctionType
AX = mybir.AxisListType


def clear_semaphores(nc, sems):
    engines = (nc.sync, nc.scalar, nc.vector, nc.gpsimd, nc.tensor)
    for n, s in enumerate(sems):
        engines[n % len(engines)].sem_clear(s)
    nc.all_engine_barrier()


def project(nc, x, w_t, pos_h_t, pos_w_t, group_mean, q_hi_d, q_lo_d, k_hi_d, k_lo_d, v_d):
    with ExitStack() as ctx:
        def sb(name, shape, dt=F32):
            return ctx.enter_context(nc.sbuf_tensor(name, shape, dt))

        def ps(name, shape):
            return ctx.enter_context(nc.psum_tensor(name, shape, F32))

        made = []

        def sem(name):
            made.append(ctx.enter_context(nc.semaphore(name)))
            return made[-1]

        xs = sb("x_sb", [P, B, CB, TP])
        w_hi = sb("w_hi", [P, CB, 3 * C], F32R)
        w_lo = sb("w_lo", [P, CB, 3 * C], F32R)
        pos_h = sb("pos_h", [P, H])
        pos_w = sb("pos_w", [P, W])
        emb = sb("emb", [P, 1, TP])
        avg = sb("avg", [P, P])
        NST = -(-T // 512)
        stats = sb("stats", [P, B * CB, NST, 6])
        mv = sb("mv", [P, B * CB, 2])
        g_mean = sb("g_mean", [P, B * CB])
        dev = sb("dev", [P, CB])
        dev2 = sb("dev2", [P, CB])
        var_e = sb("var_e", [P, CB])
        std = sb("std", [P, CB])
        r0 = sb("r0", [P, CB])
        r1 = sb("r1", [P, CB])
        r2 = sb("r2", [P, CB])
        g_rstd = sb("g_rstd", [P, B * CB])
        mean_b = sb("mean_b", [P, CB])
        rstd_b = sb("rstd_b", [P, CB])
        q_ps = ps("q_ps", [P, CB, XC])
        k_ps = ps("k_ps", [P, CB, XC])
        v_ps = ps("v_ps", [P, VT, C])
        stat_ps = ps("stat_ps", [P, 512])

        x_loaded = [sem(f"x{n}_loaded") for n in range(B * CB)]
        small_loaded = sem("small_loaded")
        w_loaded = [sem(f"w{c}_loaded") for c in range(CB)]
        w_hi_ready = sem("w_hi_ready")
        w_lo_ready = sem("w_lo_ready")
        stat_ready = sem("stat_ready")
        stat_summed = sem("stat_summed")
        std_ready = sem("std_ready")
        chain = sem("dve_chain")

        def columns(b):
            return slice(b * CB, (b + 1) * CB)

        class Chain:

            def __init__(self, dve):
                self.dve, self.links = dve, 0

            def __call__(self, ins):
                self.links += 1
                ins.then_inc(chain, 1)
                self.dve.wait_ge(chain, self.links)

        def measure(dve, link, b, c):
            n = b * CB + c
            dve.wait_ge(x_loaded[n], 16)
            for s in range(NST):
                last = nc.vector.bn_stats(stats[:, n, s, :], xs[:, b, c, s * 512:min(T, (s + 1) * 512)])
            link(last)
            last = nc.vector.bn_aggr(mv[:, n, :], stats[:, n, :, :])
            if c == CB - 1:
                last.then_inc(stat_ready, 1)

        def average_means(pe, b):
            pe.wait_ge(stat_ready, 1)
            nc.tensor.matmul(stat_ps[:, 0:CB], avg[:, :], mv[:, columns(b), 0],
                             start=True, stop=True).then_inc(stat_summed, 1)

        def deviate(dve, link, b):
            dve.wait_ge(stat_summed, 1)
            link(nc.vector.tensor_copy(g_mean[:, columns(b)], stat_ps[:, 0:CB]))
            link(nc.vector.tensor_tensor(dev[:, :], mv[:, columns(b), 0], g_mean[:, columns(b)], ALU.subtract))
            link(nc.vector.tensor_tensor(dev[:, :], dev[:, :], dev[:, :], ALU.mult))
            nc.vector.tensor_tensor(dev2[:, :], mv[:, columns(b), 1], dev[:, :], ALU.add).then_inc(stat_ready, 1)

        def average_variances(pe, b):
            pe.wait_ge(stat_ready, 2)
            nc.tensor.matmul(stat_ps[:, 0:CB], avg[:, :], dev2[:, :],
                             start=True, stop=True).then_inc(stat_summed, 1)

        def take_root(act, b):
            act.wait_ge(stat_ready, 3)
            nc.scalar.activation(std[:, :], var_e[:, :], ACT.Sqrt).then_inc(std_ready, 1)

        def invert_root(dve, link, b):
            dve.wait_ge(stat_summed, 2)
            nc.vector.tensor_scalar(var_e[:, :], stat_ps[:, 0:CB], GN_EPS, None, ALU.add).then_inc(stat_ready, 1)
            dve.wait_ge(std_ready, 1)
            link(nc.vector.reciprocal(r0[:, :], std[:, :]))
            link(nc.vector.tensor_tensor(r1[:, :], r0[:, :], r0[:, :], ALU.mult))
            link(nc.vector.tensor_tensor(r2[:, :], r1[:, :], var_e[:, :], ALU.mult))
            link(nc.vector.tensor_scalar(r1[:, :], r2[:, :], -0.5, 1.5, ALU.mult, ALU.add))
            nc.vector.tensor_tensor(g_rstd[:, columns(b)], r0[:, :], r1[:, :], ALU.mult)

        w32_scope = ExitStack()
        w32 = w32_scope.enter_context(nc.sbuf_tensor("w32", [P, CB, 3 * C], F32))

        with nc.Block() as block:
            @block.sync
            def _(sp):
                for b in range(B):
                    for c in range(CB):
                        sp.dma_start(xs[:, b, c, 0:T], x[b * CB + c, :, :]).then_inc(x_loaded[b * CB + c], 16)
                        if b == 0:
                            sp.dma_start(w32[:, c, :], w_t[c * P:(c + 1) * P, :]).then_inc(w_loaded[c], 16)
                        if b == 0 and c == 0:
                            for half in range(2):
                                rows = slice(half * D, (half + 1) * D)
                                sp.dma_start(pos_h[rows, :], pos_h_t[:, :]).then_inc(small_loaded, 16)
                                sp.dma_start(pos_w[rows, :], pos_w_t[:, :]).then_inc(small_loaded, 16)
                            sp.dma_start(avg[:, :], group_mean[:, :]).then_inc(small_loaded, 16)

            @block.scalar
            def _(act):
                for c in range(CB):
                    act.wait_ge(w_loaded[c], 16)
                    nc.scalar.copy(w_hi[:, c, :], w32[:, c, :]).then_inc(w_hi_ready, 1)
                take_root(act, 0)

            @block.gpsimd
            def _(pool):
                nc.gpsimd.memset(xs[:, :, :, T:TP], 0.0)
                nc.gpsimd.memset(emb[:, :, T:TP], 0.0)
                for c in range(CB):
                    pool.wait_ge(w_hi_ready, c + 1)
                    nc.gpsimd.tensor_tensor(w_lo[:, c, :], w32[:, c, :], w_hi[:, c, :].bitcast(F32),
                                            ALU.subtract).then_inc(w_lo_ready, 1)

            @block.tensor
            def _(pe):
                pe.wait_ge(small_loaded, 16 * 5)
                average_means(pe, 0)
                average_variances(pe, 0)

            @block.vector
            def _(dve):
                link = Chain(dve)
                for c in range(CB):
                    measure(dve, link, 0, c)
                    if c == 0:
                        dve.wait_ge(small_loaded, 16 * 5)
                        nc.vector.tensor_scalar(pos_h[:, :], pos_h[:, :], 1.0 / D, None, ALU.mult)
                        link(nc.vector.tensor_scalar(pos_w[:, :], pos_w[:, :], 1.0 / D, None, ALU.mult))
                        nc.vector.tensor_tensor(emb[:, 0, 0:T].rearrange("p (i j) -> p i j", j=W),
                                                pos_h[:, :].unsqueeze(2).broadcast_to([P, H, W]),
                                                pos_w[:, :].unsqueeze(1).broadcast_to([P, H, W]), ALU.add)
                deviate(dve, link, 0)
                invert_root(dve, link, 0)

        w32_scope.close()
        clear_semaphores(nc, made[B * CB:])

        ab_ready = sem("affine_ready")
        xn_ready = sem("xn_ready")
        xhi_ready = sem("xn_hi_ready")
        xlo_ready = sem("xn_lo_ready")
        q_made = sem("q_made")
        k_made = sem("k_made")
        v_made = sem("v_made")
        qhi_ready = sem("q_hi_ready")
        qlo_ready = sem("q_lo_ready")
        ksum_ready = sem("k_sum_ready")
        khi_ready = sem("k_hi_ready")
        klo_ready = sem("k_lo_ready")
        vhi_ready = sem("v_hi_ready")
        vlo_ready = sem("v_lo_ready")
        q_stored = sem("q_stored")
        k_stored = sem("k_stored")
        v_stored = sem("v_stored")
        xn = sb("xn", [P, CB, XC])
        xn_hi = sb("xn_hi", [P, 2, CB, XC], F32R)
        xn_lo = sb("xn_lo", [P, 2, CB, XC], F32R)
        q_hi = sb("q_hi", [P, CB, XC], F32R)
        q_lo = sb("q_lo", [P, CB, XC], F32R)
        k_sum = sb("k_sum", [P, CB, XC])
        k_hi = sb("k_hi", [P, CB, XC], F32R)
        k_lo = sb("k_lo", [P, CB, XC], F32R)
        v_parts = sb("v_parts", [P, VT, HEADS, 2, D], F32R)

        MEASURE_AT = 2
        DEVIATE_AT = MEASURE_AT + CB
        INVERT_AT_CHUNK = DEVIATE_AT + 1

        with nc.Fori(0, B) as b:
            with nc.Block() as block:
                @block.sync
                def _(sp):
                    for i in range(NXC):
                        at = slice(i * XC, (i + 1) * XC)
                        sp.wait_ge(qlo_ready, i + 1)
                        sp.dma_start(q_hi_d[bass.ds(b * CB, CB), :, at].rearrange("m p t -> p m t"),
                                     q_hi[:, :, :].bitcast(F32)).then_inc(q_stored, 16)
                        sp.dma_start(q_lo_d[bass.ds(b * CB, CB), :, at].rearrange("m p t -> p m t"),
                                     q_lo[:, :, :].bitcast(F32)).then_inc(q_stored, 16)
                        sp.wait_ge(klo_ready, i + 1)
                        sp.dma_start(k_hi_d[bass.ds(b * CB, CB), :, at].rearrange("m p t -> p m t"),
                                     k_hi[:, :, :].bitcast(F32)).then_inc(k_stored, 16)
                        sp.dma_start(k_lo_d[bass.ds(b * CB, CB), :, at].rearrange("m p t -> p m t"),
                                     k_lo[:, :, :].bitcast(F32)).then_inc(k_stored, 16)
                        sp.wait_ge(vlo_ready, i + 1)
                        for t in range(VT):
                            sp.dma_start(v_d[bass.ds(b * CB, CB), i * VT + t, :, :].rearrange("m p n -> p m n"),
                                         v_parts[:, t, :, :, :].bitcast(F32).rearrange("p (m h) s d -> p m (h s d)", m=CB)
                                         ).then_inc(v_stored, 16)
                    sp.wait_ge(q_stored, 32 * NXC)
                    sp.wait_ge(k_stored, 32 * NXC)
                    sp.wait_ge(v_stored, 16 * VT * NXC)

                @block.vector
                def _(dve):
                    nc.vector.tensor_copy(mean_b[:, :], g_mean[:, bass.ds(b * CB, CB)]).then_inc(ab_ready, 1)
                    nc.vector.tensor_copy(rstd_b[:, :], g_rstd[:, bass.ds(b * CB, CB)]).then_inc(ab_ready, 1)
                    dve.wait_ge(ab_ready, 2)

                    def normalise(i):
                        if i >= 1:
                            dve.wait_ge(xlo_ready, i)
                        for c in range(CB):
                            last = nc.vector.tensor_scalar(
                                xn[:, c, :], xs[:, bass.ds(b, 1), c, i * XC:(i + 1) * XC],
                                mean_b[:, c:c + 1], rstd_b[:, c:c + 1], ALU.subtract, ALU.mult)
                        last.then_inc(xn_ready, 1)
                        dve.wait_ge(xhi_ready, i + 1)
                        nc.vector.tensor_tensor(xn_lo[:, i % 2, :, :], xn[:, :, :],
                                                xn_hi[:, i % 2, :, :].bitcast(F32),
                                                ALU.subtract).then_inc(xlo_ready, 1)

                    link = Chain(dve)
                    normalise(0)
                    for i in range(NXC):
                        if MEASURE_AT <= i < DEVIATE_AT:
                            measure(dve, link, 1, i - MEASURE_AT)
                        if i == DEVIATE_AT:
                            deviate(dve, link, 1)
                        if i == INVERT_AT_CHUNK:
                            invert_root(dve, link, 1)
                        if i + 1 < NXC:
                            if i >= 1:
                                dve.wait_ge(v_made, i)
                            normalise(i + 1)
                        dve.wait_ge(qhi_ready, i + 1)
                        nc.vector.tensor_tensor(q_lo[:, :, :], q_ps[:, :, :], q_hi[:, :, :].bitcast(F32),
                                                ALU.subtract).then_inc(qlo_ready, 1)
                        dve.wait_ge(k_made, i + 1)
                        if i >= 1:
                            dve.wait_ge(klo_ready, i)
                        nc.vector.tensor_tensor(
                            k_sum[:, :, :], k_ps[:, :, :],
                            emb[:, :, i * XC:(i + 1) * XC].broadcast_to([P, CB, XC]),
                            ALU.add).then_inc(ksum_ready, 1)
                        dve.wait_ge(vhi_ready, i + 1)
                        nc.vector.tensor_tensor(
                            v_parts[:, :, :, 1, :],
                            v_ps[:, :, :].rearrange("p t (h d) -> p t h d", d=D),
                            v_parts[:, :, :, 0, :].bitcast(F32), ALU.subtract).then_inc(vlo_ready, 1)

                @block.scalar
                def _(act):
                    def round_x(i):
                        act.wait_ge(xn_ready, i + 1)
                        nc.scalar.copy(xn_hi[:, i % 2, :, :], xn[:, :, :]).then_inc(xhi_ready, 1)

                    round_x(0)
                    for i in range(NXC):
                        if i == INVERT_AT_CHUNK:
                            take_root(act, 1)
                        if i + 1 < NXC:
                            round_x(i + 1)
                        act.wait_ge(q_made, i + 1)
                        if i >= 1:
                            act.wait_ge(q_stored, 32 * i)
                        nc.scalar.copy(q_hi[:, :, :], q_ps[:, :, :]).then_inc(qhi_ready, 1)
                        act.wait_ge(ksum_ready, i + 1)
                        if i >= 1:
                            act.wait_ge(k_stored, 32 * i)
                        nc.scalar.copy(k_hi[:, :, :], k_sum[:, :, :]).then_inc(khi_ready, 1)
                        act.wait_ge(v_made, i + 1)
                        if i >= 1:
                            act.wait_ge(v_stored, 16 * VT * i)
                        nc.scalar.copy(v_parts[:, :, :, 0, :],
                                       v_ps[:, :, :].rearrange("p t (h d) -> p t h d", d=D)
                                       ).then_inc(vhi_ready, 1)

                @block.gpsimd
                def _(pool):
                    for i in range(NXC):
                        pool.wait_ge(khi_ready, i + 1)
                        nc.gpsimd.tensor_tensor(k_lo[:, :, :], k_sum[:, :, :], k_hi[:, :, :].bitcast(F32),
                                                ALU.subtract).then_inc(klo_ready, 1)

                @block.tensor
                def _(pe):
                    terms = [(c, w, xp) for c in range(CB)
                             for w, xp in ((w_hi, xn_hi), (w_lo, xn_hi), (w_hi, xn_lo))]

                    def channels(out, o0, i):
                        for n, (c, w, xp) in enumerate(terms):
                            last = nc.tensor.matmul(out, w[:, c, o0:o0 + P], xp[:, i % 2, c, :],
                                                    start=(n == 0), stop=(n == len(terms) - 1))
                        return last

                    for i in range(NXC):
                        if i == DEVIATE_AT:
                            average_means(pe, 1)
                        if i == INVERT_AT_CHUNK:
                            average_variances(pe, 1)
                        pe.wait_ge(xlo_ready, i + 1)
                        if i >= 1:
                            pe.wait_ge(qlo_ready, i)
                        for m in range(CB):
                            last = channels(q_ps[:, m, :], m * P, i)
                        last.then_inc(q_made, 1)
                        if i >= 1:
                            pe.wait_ge(ksum_ready, i)
                        for m in range(CB):
                            last = channels(k_ps[:, m, :], C + m * P, i)
                        last.then_inc(k_made, 1)
                        if i >= 1:
                            pe.wait_ge(vlo_ready, i)
                        for t in range(VT):
                            for n, (c, w, xp) in enumerate(terms):
                                last = nc.tensor.matmul(v_ps[:, t, :], xp[:, i % 2, c, t * P:(t + 1) * P],
                                                        w[:, c, 2 * C:3 * C],
                                                        start=(n == 0), stop=(n == len(terms) - 1))
                        last.then_inc(v_made, 1)

            clear_semaphores(nc, made[B * CB:])



FIRST_TILE = LEAD // TILE_STEPS
LOAD_EVERY = 3
TURN_PAIRS = 2
START = 18
NP, NHI, NLO = 4, 6, 6
SUM_LAG = 1
BANKS = 3
SUMMED = UNIT_STEPS - 1
BOTH_AT = 1
TOTAL_AT = LAG - 2
LAST_AT = (LAG - 1, LAG)
TOTAL_READ_AT = LAG + 1
TOTAL_FREE_AT = LAG + 1
INVERT_AT, FINISH_AT = 10, 15
INV_COLS = 10
INV_ROWS = 2 * QB // INV_COLS


def is_added(g):
    return 1 <= g % UNIT_STEPS < SUMMED


def sums_before(g):
    unit, t = divmod(g, UNIT_STEPS)
    return unit * (SUMMED - 1) + min(max(t - 1, 0), SUMMED - 1)


def sums_through(g):
    return sums_before(g + 2 if g % UNIT_STEPS == 0 else g + 1)


def key_tiles(g):
    t = g % UNIT_STEPS
    return [(a, 2 * t + a, LAST_KEYS if 2 * t + a == KT - 1 else P) for a in range(2)]


class Ring:

    def __init__(self, steps, chunk_steps, units):
        self.chunks, self.totals = {}, {}
        self.before = {}
        taken, last_job = list(range(BANKS)), {}
        for g in steps:
            unit, t = divmod(g, UNIT_STEPS)
            held = self.totals.get(unit - 1) if t <= TOTAL_FREE_AT else None
            turn = g - steps[0]
            jobs = [("chunk", 2 * turn + 1), ("chunk", 2 * turn + 2)] if g in chunk_steps else []
            if 1 <= unit <= units and t == TOTAL_AT:
                jobs.append(("total", len(self.totals) + 1))
            banks = {}
            for job in jobs:
                bank = next(b for b in taken if b != held)
                taken.remove(bank)
                taken.append(bank)
                self.before[job] = last_job.get(bank)
                banks[job] = bank
                last_job[bank] = job
                if job[0] == "total":
                    held = self.totals[unit - 1] = bank
            if g in chunk_steps:
                self.chunks[g] = (banks[jobs[0]], banks[jobs[1]])


def attend(nc, x, out, q_hi_d, q_lo_d, k_hi_d, k_lo_d, v_d, inv_d):
    with ExitStack() as ctx:
        def sb(name, shape, dt=F32):
            return ctx.enter_context(nc.sbuf_tensor(name, shape, dt))

        def ps(name, shape):
            return ctx.enter_context(nc.psum_tensor(name, shape, F32))

        made = []

        def sem(name):
            made.append(ctx.enter_context(nc.semaphore(name)))
            return made[-1]

        k_parts = [sb(f"k_parts{h}", [P, TP], F32R) for h in range(2)]
        k_one = [sb(f"k_one{h}", [D + 1, TP], F32R) for h in range(2)]
        q_twice = [sb(f"q_twice{h}", [P, TQ], F32R) for h in range(2)]
        q_max = [sb(f"q_max{h}", [D + 1, TQ], F32R) for h in range(2)]
        v_parts = [sb(f"v_parts{h}", [P, KT, 2 * D], F32R) for h in range(2)]
        probs = sb("probs", [P, NP, 2, QB])
        p_hi = sb("p_hi", [P, NHI, 2, QB], F32R)
        p_lo = sb("p_lo", [P, NLO, 2, QB], F32R)
        sums = sb("sums", [P, 2, 2, QB])
        sums_both = sb("sums_both", [P, QB])
        by_v_hi = sb("by_v_hi", [P, QB])
        by_v_lo = sb("by_v_lo", [P, QB])
        totals = sb("totals", [P, QB])
        tot_cols = sb("tot_cols", [INV_ROWS, INV_COLS])
        inv_cols = sb("inv_cols", [INV_ROWS, INV_COLS])
        inv_total = sb("inv_total", [P, QB])
        x_res = sb("x_res", [P, 2, QB])
        result = sb("result", [P, 2, QB])
        part_max = sb("part_max", [P, 2, MAX_CHUNKS])
        neg_max = sb("neg_max", [P, 2], F32R)
        ones = sb("ones", [P, D])
        ones_r = sb("ones_r", [P, D], F32R)

        scores_ps = ps("scores_ps", [P, 2, 2, 512])
        out_ps = ps("out_ps", [P, 512])
        ring_ps = ps("ring_ps", [P, BANKS, 512])

        loads = [sem(f"head{h}_q_hi_and_k_loaded") for h in range(2)]
        rest_loads = [sem(f"head{h}_rest_loaded") for h in range(2)]
        const_set = sem("const_set")
        x_loaded = [sem(f"x_res{r}_loaded") for r in range(2)]
        stored = [sem(f"result{r}_stored") for r in range(2)]
        scores_made = sem("scores_made")
        probs_made = sem("probs_made")
        hi_made = sem("p_hi_made")
        lo_made = sem("p_lo_made")
        summed = sem("summed")
        both_summed = sem("sums_both_made")
        pv_made = sem("pv_made")
        chunks_made = sem("chunks_made")
        chunks_read = sem("chunks_read")
        total_made = sem("total_made")
        total_read = sem("total_read")
        max_made = sem("neg_max_made")
        row_written = sem("max_row_written")
        copied = sem("out_ps_copied")
        folded = sem("folded")
        weighed = sem("weighed")
        added = sem("added")
        tot_spread = sem("tot_cols_loaded")
        inverted = sem("inverted")
        inv_stored = sem("inv_stored")
        inv_loaded = sem("inv_total_loaded")

        def load_part(eng, h, pair, part):
            loaded = (loads if part < FIRST_PARTS else rest_loads)[h]
            rows = slice(h * D, (h + 1) * D)
            if part == 6:
                return eng.dma_start(v_parts[h][:, :, :].bitcast(F32),
                                     v_d[bass.ds(pair, 1), :, :, h * 2 * D:(h + 1) * 2 * D]
                                     .rearrange("o k p n -> p (o k) n")).then_inc(loaded, 16)
            where, what = ((k_parts[h][0:D, :], k_hi_d), (k_parts[h][D:P, :], k_lo_d),
                           (q_twice[h][0:D, 0:TP], q_hi_d), (q_twice[h][D:P, 0:TP], q_hi_d),
                           (k_one[h][0:D, :], k_hi_d), (q_max[h][0:D, 0:TP], q_lo_d))[part]
            return eng.dma_start(where.bitcast(F32),
                                 what[bass.ds(pair, 1), rows, :].rearrange("o p t -> (o p) t")
                                 ).then_inc(loaded, 16)

        PARTS = 7
        FIRST_PARTS = 4
        FIRST_LOADED, REST_LOADED = 16 * FIRST_PARTS, 16 * (PARTS - FIRST_PARTS)

        def tile_of(tile):
            return (tile // KT) % 2, tile % KT

        def block_of(unit):
            q0 = (unit % UNITS) * QB
            return (unit // UNITS) % 2, q0, min(QB, T - q0)

        def fill_chunk(bank, g, second):
            tile, third = divmod(g + LEAD, TILE_STEPS)
            h, t = tile_of(tile)
            k0 = min((CHUNKS_A_STEP * third + second) * QB, T - QB)
            return nc.tensor.matmul(ring_ps[:, bank, 0:QB], q_twice[h][:, t * P:(t + 1) * P],
                                    k_parts[h][:, k0:k0 + QB], start=True, stop=True)

        def read_chunk(bank, g, second):
            tile, third = divmod(g + LEAD, TILE_STEPS)
            part = CHUNKS_A_STEP * third + second
            return nc.vector.reduce_max(part_max[:, tile % 2, part:part + 1], ring_ps[:, bank, 0:QB], AX.X)

        def finish_tile(tile):
            return nc.vector.tensor_reduce(neg_max[:, tile % 2:tile % 2 + 1], part_max[:, tile % 2, :],
                                           AX.X, ALU.max, negate=True)

        def write_row(sp, tile):
            h, t = tile_of(tile)
            return sp.dma_start(q_max[h][D:D + 1, t * P:(t + 1) * P].bitcast(F32),
                                neg_max[:, tile % 2:tile % 2 + 1].bitcast(F32))

        with nc.Block() as block:
            fills = [(ones[:, :], 1.0), (x_res[:, :, :], 0.0)]
            for h in range(2):
                fills += [(k_one[h][D:D + 1, :].bitcast(F32), 1.0),
                          (q_twice[h][:, TP:TQ].bitcast(F32), 0.0),
                          (q_max[h][:, TP:TQ].bitcast(F32), 0.0)]

            @block.sync
            def _(sp):
                for part in range(PARTS):
                    load_part(sp, 0, 0, part)
                sp.wait_ge(rest_loads[0], REST_LOADED)
                sp.wait_ge(const_set, len(fills) + 1)
                for tile in range(FIRST_TILE):
                    sp.wait_ge(max_made, tile + 1)
                    write_row(sp, tile).then_inc(row_written, 16)
                    sp.wait_ge(row_written, 16 * (tile + 1))

            @block.gpsimd
            def _(pool):
                for n, (where, value) in enumerate(fills):
                    if n >= 1:
                        pool.wait_ge(const_set, n)
                    nc.gpsimd.memset(where, value).then_inc(const_set, 1)
                pool.wait_ge(const_set, len(fills))
                nc.gpsimd.tensor_copy(ones_r[:, :], ones[:, :]).then_inc(const_set, 1)

            @block.tensor
            def _(pe):
                pe.wait_ge(loads[0], FIRST_LOADED)
                for n in range(2 * LEAD):
                    if n >= BANKS:
                        pe.wait_ge(chunks_read, n - BANKS + 1)
                    fill_chunk(n % BANKS, n // 2 - LEAD, n % 2).then_inc(chunks_made, 1)

            @block.vector
            def _(dve):
                for n in range(2 * LEAD):
                    tile, part = divmod(n, MAX_CHUNKS)
                    dve.wait_ge(chunks_made, n + 1)
                    read_chunk(n % BANKS, n // 2 - LEAD, n % 2).then_inc(chunks_read, 1)
                    if part == MAX_CHUNKS - 1:
                        dve.wait_ge(chunks_read, n + 1)
                        if tile >= 2:
                            dve.wait_ge(row_written, 16 * (tile - 1))
                        finish_tile(tile).then_inc(max_made, 1)

        clear_semaphores(nc, made)

        def run_steps(block, begin, end, pair, made_end=None):
            last_turn = made_end is not None
            made_end = made_end if last_turn else end + LEAD
            steps = range(begin, end)
            chunk_steps = range(begin, min(end, made_end - LEAD))
            units = made_end // UNIT_STEPS
            ring = Ring(steps, chunk_steps, units)
            probs_before = begin
            hi_before = max(0, begin - HI_LAG)
            lo_before = max(0, begin - LO_LAG)
            summed_before = sums_before(max(0, begin - SUM_LAG))
            pv_before = max(0, begin - LAG)
            totals_before = (begin - TOTAL_AT - 1) // UNIT_STEPS if begin else 0
            copies_before = (begin - LAG - 1) // UNIT_STEPS if begin else 0
            tiles_before = (begin - 1 + LEAD) // TILE_STEPS if begin else FIRST_TILE

            def multiply_v(pe, s):
                if not 0 <= s < made_end:
                    return
                unit, t = divmod(s, UNIT_STEPS)
                if s >= lo_before:
                    pe.wait_ge(lo_made, s + 1 - lo_before)
                if t == 0 and unit > copies_before:
                    pe.wait_ge(copied, 2 * (unit - copies_before))
                for a, kt, rows in key_tiles(s):
                    v_tile = v_parts[block_of(unit)[0]][0:rows, kt, :]
                    nc.tensor.matmul(out_ps[:, 0:QB], v_tile, p_hi[0:rows, s % NHI, a, :],
                                     start=(kt == 0), stop=False)
                    last = nc.tensor.matmul(out_ps[:, 0:QB], v_tile, p_lo[0:rows, s % NLO, a, :],
                                            start=False, stop=(kt == KT - 1))
                last.then_inc(pv_made, 1)

            def total_sums(pe, unit):
                pe.wait_ge(both_summed, unit + 1 - totals_before)
                nc.tensor.matmul(ring_ps[0:D, ring.totals[unit], 0:QB], ones[:, :], sums_both[:, :],
                                 start=True, stop=False)

            def total_last(pe, unit, a):
                s = unit * UNIT_STEPS + SUMMED
                _, kt, rows = key_tiles(s)[a]
                where = ring_ps[0:D, ring.totals[unit], 0:QB]
                nc.tensor.matmul(where, ones_r[0:rows, :], p_hi[0:rows, s % NHI, a, :], start=False, stop=False)
                last = nc.tensor.matmul(where, ones_r[0:rows, :], p_lo[0:rows, s % NLO, a, :],
                                        start=False, stop=(kt == KT - 1))
                if kt == KT - 1:
                    last.then_inc(total_made, 1)

            @block.tensor
            def _(pe):
                def bank_freed(job):
                    if ring.before[job] is not None:
                        kind, count = ring.before[job]
                        pe.wait_ge(chunks_read if kind == "chunk" else total_read, count)

                def make_scores(g):
                    unit, t = divmod(g, UNIT_STEPS)
                    h, q0, _ = block_of(unit)
                    if g - 1 > probs_before:
                        pe.wait_ge(probs_made, g - 1 - probs_before)
                    if t == 0 and unit % UNITS == 0 and unit:
                        head = unit // UNITS
                        pe.wait_ge(rest_loads[head % 2], REST_LOADED * ((head + 1) // 2))
                    if t == 0:
                        tile = unit // UNITS * KT + min(KT, -(-(q0 + QB) // P)) - 1
                        if tile >= tiles_before:
                            pe.wait_ge(row_written, 16 * (tile + 1 - tiles_before))
                    for a, kt, _ in key_tiles(g):
                        keys = slice(kt * P, (kt + 1) * P)
                        where = scores_ps[:, g % 2, a, 0:QB]
                        nc.tensor.matmul(where, k_parts[h][:, keys], q_twice[h][:, q0:q0 + QB],
                                         start=True, stop=False)
                        last = nc.tensor.matmul(where, k_one[h][:, keys], q_max[h][:, q0:q0 + QB],
                                                start=False, stop=True)
                    last.then_inc(scores_made, 1)

                for g in steps:
                    unit, t = divmod(g, UNIT_STEPS)
                    if g < made_end:
                        make_scores(g)
                    turn = g - begin
                    head, first = divmod(g + LEAD, HEAD_STEPS)
                    if g in chunk_steps and first == 0:
                        pe.wait_ge(loads[head % 2], FIRST_LOADED * ((head + 1) // 2))
                    if g in chunk_steps:
                        bank_freed(("chunk", 2 * turn + 1))
                        fill_chunk(ring.chunks[g][0], g, 0).then_inc(chunks_made, 1)
                    if t == LAG + 1:
                        multiply_v(pe, g - LAG - 1)
                    if t != LAG:
                        multiply_v(pe, g - LAG)
                    if g in chunk_steps:
                        bank_freed(("chunk", 2 * turn + 2))
                        fill_chunk(ring.chunks[g][1], g, 1).then_inc(chunks_made, 1)
                    if 1 <= unit <= units and t == TOTAL_AT:
                        bank_freed(("total", unit - totals_before))
                        total_sums(pe, unit - 1)
                    for a in range(2):
                        if 1 <= unit <= units and t == LAST_AT[a]:
                            total_last(pe, unit - 1, a)

            @block.scalar
            def _(act):
                for g in steps:
                    unit, t = divmod(g, UNIT_STEPS)
                    s = g - HI_LAG
                    if 0 <= s < made_end:
                        if s >= probs_before:
                            act.wait_ge(probs_made, s + 1 - probs_before)
                        if s - NHI >= pv_before:
                            act.wait_ge(pv_made, s - NHI + 1 - pv_before)
                        over = s - NHI
                        if over >= 0 and over % UNIT_STEPS == SUMMED and over // UNIT_STEPS >= totals_before:
                            act.wait_ge(total_made, over // UNIT_STEPS + 1 - totals_before)
                        nc.scalar.copy(p_hi[:, s % NHI, :, :], probs[:, s % NP, :, :]).then_inc(hi_made, 1)
                    if g < made_end:
                        act.wait_ge(scores_made, g + 1 - begin)
                        if g - NP >= lo_before:
                            act.wait_ge(lo_made, g - NP + 1 - lo_before)
                        if g >= NP and sums_through(g - NP) > summed_before:
                            act.wait_ge(summed, sums_through(g - NP) - summed_before)
                        nc.scalar.activation(probs[:, g % NP, :, :], scores_ps[:, g % 2, :, 0:QB],
                                             ACT.Exp, scale=float(D) ** 0.5).then_inc(probs_made, 1)
                    if 1 <= unit <= units and t == LAG:
                        u = unit - 1
                        act.wait_ge(pv_made, unit * UNIT_STEPS - pv_before)
                        if u >= 2 and u % 2 == 0:
                            act.wait_ge(folded, u // 2)
                        to = slice((u % 2) * D, (u % 2 + 1) * D)
                        nc.scalar.copy(by_v_hi[to, :], out_ps[0:D, 0:QB]).then_inc(copied, 1)
                        nc.scalar.copy(by_v_lo[to, :], out_ps[D:P, 0:QB]).then_inc(copied, 1)
                    if 1 <= unit <= units and t == TOTAL_READ_AT:
                        u = unit - 1
                        act.wait_ge(total_made, unit - totals_before)
                        if u >= 2 and u % 2 == 0:
                            act.wait_ge(tot_spread, 16 * (u // 2))
                        nc.scalar.copy(totals[(u % 2) * D:(u % 2 + 1) * D, :], ring_ps[0:D, ring.totals[u], 0:QB]
                                       ).then_inc(total_read, 1)

            @block.gpsimd
            def _(pool):
                for s in range(lo_before, min(end - LO_LAG, made_end)):
                    if s >= hi_before:
                        pool.wait_ge(hi_made, s + 1 - hi_before)
                    over = s - NLO
                    if over >= pv_before:
                        pool.wait_ge(pv_made, over + 1 - pv_before)
                    if over >= 0 and over % UNIT_STEPS == SUMMED and over // UNIT_STEPS >= totals_before:
                        pool.wait_ge(total_made, over // UNIT_STEPS + 1 - totals_before)
                    nc.gpsimd.tensor_tensor(p_lo[:, s % NLO, :, :], probs[:, s % NP, :, :],
                                            p_hi[:, s % NHI, :, :].bitcast(F32),
                                            ALU.subtract).then_inc(lo_made, 1)

            @block.vector
            def _(dve):
                def add_sums(s):
                    unit, t = divmod(s, UNIT_STEPS)
                    if not 0 <= s < made_end or not is_added(s):
                        return
                    if s >= probs_before:
                        dve.wait_ge(probs_made, s + 1 - probs_before)
                    first = sums[:, unit % 2, :, :]
                    if t == 1:
                        first = probs[:, (s - 1) % NP, :, :]
                    elif sums_before(s) > summed_before:
                        dve.wait_ge(summed, sums_before(s) - summed_before)
                    nc.vector.tensor_tensor(sums[:, unit % 2, :, :], first, probs[:, s % NP, :, :],
                                            ALU.add).then_inc(summed, 1)

                for g in steps:
                    unit, t = divmod(g, UNIT_STEPS)
                    duo, at = divmod(g, DUO)
                    done = duo - 1
                    turn = g - begin
                    if g in chunk_steps:
                        dve.wait_ge(chunks_made, 2 * turn + 1)
                        read_chunk(ring.chunks[g][0], g, 0).then_inc(chunks_read, 1)
                    tile, third = divmod(g + LEAD, TILE_STEPS)
                    tile -= 1
                    if third == 0 and tile >= tiles_before and g + LEAD <= made_end:
                        dve.wait_ge(chunks_read, 2 * turn)
                        if tile - 2 >= tiles_before:
                            dve.wait_ge(row_written, 16 * (tile - 1 - tiles_before))
                        finish_tile(tile).then_inc(max_made, 1)
                    add_sums(g - SUM_LAG)
                    if 1 <= unit <= units and t == BOTH_AT:
                        dve.wait_ge(summed, unit * (SUMMED - 1) - summed_before)
                        if unit - 1 > totals_before:
                            dve.wait_ge(total_made, unit - 1 - totals_before)
                        nc.vector.tensor_tensor(sums_both[:, :], sums[:, (unit - 1) % 2, 0, :],
                                                sums[:, (unit - 1) % 2, 1, :], ALU.add).then_inc(both_summed, 1)
                    if g in chunk_steps:
                        dve.wait_ge(chunks_made, 2 * turn + 2)
                        read_chunk(ring.chunks[g][1], g, 1).then_inc(chunks_read, 1)
                    if pair is None or duo < 1:
                        continue
                    r = done % 2
                    if at == INVERT_AT:
                        dve.wait_ge(tot_spread, 16 * duo)
                        if duo >= 2:
                            dve.wait_ge(inv_stored, 16 * done)
                        nc.vector.reciprocal(inv_cols[:, :], tot_cols[:, :]).then_inc(inverted, 1)
                    if at == FINISH_AT - 3:
                        dve.wait_ge(copied, 2 * (2 * duo - copies_before))
                        if done >= 2:
                            dve.wait_ge(stored[r], 32 * (done // 2))
                        nc.vector.tensor_tensor(result[:, r, :], by_v_hi[:, :], by_v_lo[:, :],
                                                ALU.add).then_inc(folded, 1)
                    if at == FINISH_AT - 1:
                        dve.wait_ge(folded, duo)
                        dve.wait_ge(inv_loaded, 32 * duo)
                        nc.vector.tensor_tensor(result[:, r, :], result[:, r, :], inv_total[:, :],
                                                ALU.mult).then_inc(weighed, 1)
                    if at == FINISH_AT:
                        dve.wait_ge(weighed, duo)
                        dve.wait_ge(x_loaded[r], 32 * (done // 2 + 1))
                        nc.vector.tensor_tensor(result[:, r, :], result[:, r, :], x_res[:, r, :],
                                                ALU.add).then_inc(added, 1)

            @block.sync
            def _(sp):
                for g in steps:
                    duo, at = divmod(g, DUO)
                    done = duo - 1
                    tile, third = divmod(g + LEAD, TILE_STEPS)
                    if third == 0 and tile - 1 >= tiles_before and g + LEAD <= made_end:
                        sp.wait_ge(max_made, tile - tiles_before)
                        write_row(sp, tile - 1).then_inc(row_written, 16)
                        sp.wait_ge(row_written, 16 * (tile - tiles_before))
                    if pair is None:
                        continue
                    if g == begin or at == 0 and 1 <= duo < TURN_PAIRS * DUOS:
                        if duo >= 2:
                            sp.wait_ge(added, duo - 1)
                        for half in range(2):
                            h, q, width = block_of(2 * duo + half)
                            sp.dma_start(x_res[half * D:(half + 1) * D, duo % 2, 0:width],
                                         x[bass.ds(pair + 2 * duo // PAIR_UNITS, 1), h * D:(h + 1) * D, q:q + width]
                                         .rearrange("o p t -> (o p) t")).then_inc(x_loaded[duo % 2], 16)
                    for head in range(1, 2 * TURN_PAIRS + 1 - last_turn):
                        free_at = max(begin, (head - 1) * HEAD_STEPS + LAG)
                        part, off = divmod(g - free_at, LOAD_EVERY)
                        if off == 0 and 0 <= part < PARTS:
                            if part == 0 and head >= 2:
                                sp.wait_ge(pv_made, (head - 1) * HEAD_STEPS - pv_before)
                            load_part(sp, head % 2, pair + head // 2, part)
                    if duo >= 1 and at == INVERT_AT - 2:
                        sp.wait_ge(total_read, 2 * duo - totals_before)
                        if duo >= 2:
                            sp.wait_ge(inverted, done)
                        sp.dma_start(tot_cols[:, :], totals[0:P:D, :].rearrange("a (r c) -> a r c", c=INV_COLS)
                                     ).then_inc(tot_spread, 16)
                    if duo >= 1 and at == INVERT_AT:
                        sp.wait_ge(inverted, duo)
                        if duo >= 2:
                            sp.wait_ge(inv_loaded, 32 * done)
                        sp.dma_start(inv_d[0, :].rearrange("(r c) -> r c", c=INV_COLS), inv_cols[:, :]
                                     ).then_inc(inv_stored, 16)
                        sp.wait_ge(inv_stored, 16 * duo)
                        if duo >= 2:
                            sp.wait_ge(weighed, done)
                        for half in range(2):
                            sp.dma_start(inv_total[half * D:(half + 1) * D, :],
                                         inv_d[:, half * QB:(half + 1) * QB].broadcast_to([D, QB])
                                         ).then_inc(inv_loaded, 16)
                    if duo >= 1 and at == FINISH_AT:
                        sp.wait_ge(added, duo)
                        for half in range(2):
                            h, q, width = block_of(2 * done + half)
                            sp.dma_start(out[bass.ds(pair + 2 * done // PAIR_UNITS, 1), h * D:(h + 1) * D, q:q + width]
                                         .rearrange("o p t -> (o p) t"),
                                         result[half * D:(half + 1) * D, done % 2, 0:width]
                                         ).then_inc(stored[done % 2], 16)
                if pair is not None:
                    for r in range(2):
                        sp.wait_ge(stored[r], 32 * TURN_PAIRS * DUOS // 2)
                    for h, heads in enumerate((TURN_PAIRS - last_turn, TURN_PAIRS)):
                        sp.wait_ge(loads[h], FIRST_LOADED * heads)
                        sp.wait_ge(rest_loads[h], REST_LOADED * heads)

        with nc.Block() as block:
            run_steps(block, 0, START, None)

        clear_semaphores(nc, made)

        with nc.Fori(0, PAIRS // TURN_PAIRS - 1) as turn:
            with nc.Block() as block:
                run_steps(block, START, START + TURN_PAIRS * STEPS, turn * TURN_PAIRS)

            clear_semaphores(nc, made)

        with nc.Block() as block:
            run_steps(block, START, TURN_PAIRS * STEPS + FINISH_AT + 1, PAIRS - TURN_PAIRS, TURN_PAIRS * STEPS)


def attention_block(nc, x, w_t, pos_h_t, pos_w_t, group_mean, out):
    q_hi_d = nc.dram_tensor("q_hi_d", [PAIRS, P, TP], F32, kind="Internal").ap()
    q_lo_d = nc.dram_tensor("q_lo_d", [PAIRS, P, TP], F32, kind="Internal").ap()
    k_hi_d = nc.dram_tensor("k_hi_d", [PAIRS, P, TP], F32, kind="Internal").ap()
    k_lo_d = nc.dram_tensor("k_lo_d", [PAIRS, P, TP], F32, kind="Internal").ap()
    v_d = nc.dram_tensor("v_d", [PAIRS, KT, P, 4 * D], F32, kind="Internal").ap()
    inv_d = nc.dram_tensor("inv_d", [1, 2 * QB], F32, kind="Internal").ap()
    project(nc, x, w_t, pos_h_t, pos_w_t, group_mean, q_hi_d, q_lo_d, k_hi_d, k_lo_d, v_d)
    attend(nc, x, out, q_hi_d, q_lo_d, k_hi_d, k_lo_d, v_d, inv_d)


def kernel(**inputs):
    import concourse.bacc as bacc
    from concourse.bass_utils import run_bass_kernel_spmd

    x = np.ascontiguousarray(inputs["x"]).reshape(PAIRS, P, T)
    arrays = {
        "in_x": x,
        "in_w_t": np.ascontiguousarray(np.asarray(inputs["L0_conv_w_in"]).T),
        "in_pos_h_t": np.ascontiguousarray(np.asarray(inputs["L0_conv_pos_h"]).T),
        "in_pos_w_t": np.ascontiguousarray(np.asarray(inputs["L0_conv_pos_w"]).T),
        "in_group_mean": np.kron(np.eye(P // GROUP, dtype=np.float32),
                                 np.full((GROUP, GROUP), 1.0 / GROUP, np.float32)),
    }
    nc = bacc.Bacc("TRN2", target_bir_lowering=False, num_devices=1)
    args = [nc.dram_tensor(n, a.shape, F32, kind="ExternalInput").ap() for n, a in arrays.items()]
    out = nc.dram_tensor("out", [PAIRS, P, T], F32, kind="ExternalOutput").ap()
    attention_block(nc, *args, out)
    r = run_bass_kernel_spmd(nc, [arrays], core_ids=[0])
    return r.results[0]["out"].reshape(B, C, H, W)
```
